# Optimizing a Trainium2 kernel written in Bass

```python
import numpy as np
import jax
import jax.numpy as jnp

def _softmax(x, axis=-1):
    return jax.nn.softmax(x, axis=axis)

def _gelu(x):
    return jax.nn.gelu(x, approximate=True)

def _silu(x):
    return jax.nn.silu(x)

def _sigmoid(x):
    return jax.nn.sigmoid(x)

def _layernorm(x, axis=-1, eps=1e-05):
    m = jnp.mean(x, axis=axis, keepdims=True)
    v = jnp.var(x, axis=axis, keepdims=True)
    return (x - m) / jnp.sqrt(v + eps)

def _scatter_add(tgt, idx, src, axis=0):
    return tgt.at[idx].add(src)

def _segment_sum(src, seg, n):
    return jax.ops.segment_sum(src, seg, n)
kernel_name = 'mk_dlrm_tower_d1_rec_r8_be330f'

def setup_inputs(seed: int=0):
    np.random.seed(seed)
    _w = jnp.asarray

    def _rec_inputs():
        import jax
        import jax.numpy as jnp
        _tk = jax.random.key(seed)
        dense_ctx = jax.random.normal(jax.random.fold_in(_tk, 190), (512, 16), jnp.float32)
        ids = jnp.stack([jax.random.randint(jax.random.fold_in(_tk, 200 + f), (512,), 0, v, jnp.int32) for f, v in enumerate([1250, 1250, 125000, 1250, 1000, 1000, 12500, 1250, 12500, 125000, 125000, 1250, 12500, 1250, 12500, 1000, 12500, 1250, 1250, 12500, 1250, 1250, 1000, 125000, 12500, 1250, 1250, 12500, 1000, 125000, 125000, 125000, 1000, 1250, 125000, 125000, 12500, 12500, 12500])], axis=1)
        tbl_0 = 0.05 * jax.random.normal(jax.random.fold_in(_tk, 500 + 0), (1250, 16), jnp.float32)
        tbl_1 = 0.05 * jax.random.normal(jax.random.fold_in(_tk, 500 + 1), (1250, 16), jnp.float32)
        tbl_2 = 0.05 * jax.random.normal(jax.random.fold_in(_tk, 500 + 2), (125000, 16), jnp.float32)
        tbl_3 = 0.05 * jax.random.normal(jax.random.fold_in(_tk, 500 + 3), (1250, 16), jnp.float32)
        tbl_4 = 0.05 * jax.random.normal(jax.random.fold_in(_tk, 500 + 4), (1000, 16), jnp.float32)
        tbl_5 = 0.05 * jax.random.normal(jax.random.fold_in(_tk, 500 + 5), (1000, 16), jnp.float32)
        tbl_6 = 0.05 * jax.random.normal(jax.random.fold_in(_tk, 500 + 6), (12500, 16), jnp.float32)
        tbl_7 = 0.05 * jax.random.normal(jax.random.fold_in(_tk, 500 + 7), (1250, 16), jnp.float32)
        tbl_8 = 0.05 * jax.random.normal(jax.random.fold_in(_tk, 500 + 8), (12500, 16), jnp.float32)
        tbl_9 = 0.05 * jax.random.normal(jax.random.fold_in(_tk, 500 + 9), (125000, 16), jnp.float32)
        tbl_10 = 0.05 * jax.random.normal(jax.random.fold_in(_tk, 500 + 10), (125000, 16), jnp.float32)
        tbl_11 = 0.05 * jax.random.normal(jax.random.fold_in(_tk, 500 + 11), (1250, 16), jnp.float32)
        tbl_12 = 0.05 * jax.random.normal(jax.random.fold_in(_tk, 500 + 12), (12500, 16), jnp.float32)
        tbl_13 = 0.05 * jax.random.normal(jax.random.fold_in(_tk, 500 + 13), (1250, 16), jnp.float32)
        tbl_14 = 0.05 * jax.random.normal(jax.random.fold_in(_tk, 500 + 14), (12500, 16), jnp.float32)
        tbl_15 = 0.05 * jax.random.normal(jax.random.fold_in(_tk, 500 + 15), (1000, 16), jnp.float32)
        tbl_16 = 0.05 * jax.random.normal(jax.random.fold_in(_tk, 500 + 16), (12500, 16), jnp.float32)
        tbl_17 = 0.05 * jax.random.normal(jax.random.fold_in(_tk, 500 + 17), (1250, 16), jnp.float32)
        tbl_18 = 0.05 * jax.random.normal(jax.random.fold_in(_tk, 500 + 18), (1250, 16), jnp.float32)
        tbl_19 = 0.05 * jax.random.normal(jax.random.fold_in(_tk, 500 + 19), (12500, 16), jnp.float32)
        tbl_20 = 0.05 * jax.random.normal(jax.random.fold_in(_tk, 500 + 20), (1250, 16), jnp.float32)
        tbl_21 = 0.05 * jax.random.normal(jax.random.fold_in(_tk, 500 + 21), (1250, 16), jnp.float32)
        tbl_22 = 0.05 * jax.random.normal(jax.random.fold_in(_tk, 500 + 22), (1000, 16), jnp.float32)
        tbl_23 = 0.05 * jax.random.normal(jax.random.fold_in(_tk, 500 + 23), (125000, 16), jnp.float32)
        tbl_24 = 0.05 * jax.random.normal(jax.random.fold_in(_tk, 500 + 24), (12500, 16), jnp.float32)
        tbl_25 = 0.05 * jax.random.normal(jax.random.fold_in(_tk, 500 + 25), (1250, 16), jnp.float32)
        tbl_26 = 0.05 * jax.random.normal(jax.random.fold_in(_tk, 500 + 26), (1250, 16), jnp.float32)
        tbl_27 = 0.05 * jax.random.normal(jax.random.fold_in(_tk, 500 + 27), (12500, 16), jnp.float32)
        tbl_28 = 0.05 * jax.random.normal(jax.random.fold_in(_tk, 500 + 28), (1000, 16), jnp.float32)
        tbl_29 = 0.05 * jax.random.normal(jax.random.fold_in(_tk, 500 + 29), (125000, 16), jnp.float32)
        tbl_30 = 0.05 * jax.random.normal(jax.random.fold_in(_tk, 500 + 30), (125000, 16), jnp.float32)
        tbl_31 = 0.05 * jax.random.normal(jax.random.fold_in(_tk, 500 + 31), (125000, 16), jnp.float32)
        tbl_32 = 0.05 * jax.random.normal(jax.random.fold_in(_tk, 500 + 32), (1000, 16), jnp.float32)
        tbl_33 = 0.05 * jax.random.normal(jax.random.fold_in(_tk, 500 + 33), (1250, 16), jnp.float32)
        tbl_34 = 0.05 * jax.random.normal(jax.random.fold_in(_tk, 500 + 34), (125000, 16), jnp.float32)
        tbl_35 = 0.05 * jax.random.normal(jax.random.fold_in(_tk, 500 + 35), (125000, 16), jnp.float32)
        tbl_36 = 0.05 * jax.random.normal(jax.random.fold_in(_tk, 500 + 36), (12500, 16), jnp.float32)
        tbl_37 = 0.05 * jax.random.normal(jax.random.fold_in(_tk, 500 + 37), (12500, 16), jnp.float32)
        tbl_38 = 0.05 * jax.random.normal(jax.random.fold_in(_tk, 500 + 38), (12500, 16), jnp.float32)
        _rk = jax.random.fold_in(_tk, 7)
        W_top1 = 0.05 * jax.random.normal(jax.random.fold_in(_tk, 801), (400, 512), jnp.float32)
        W_top2 = 0.0441942 * jax.random.normal(jax.random.fold_in(_tk, 802), (512, 256), jnp.float32)
        W_top3 = 0.0625 * jax.random.normal(jax.random.fold_in(_tk, 803), (256, 1), jnp.float32)
        b_top1 = jnp.zeros((512,), jnp.float32)
        b_top2 = jnp.zeros((256,), jnp.float32)
        return (dense_ctx, ids, tbl_0, tbl_1, tbl_2, tbl_3, tbl_4, tbl_5, tbl_6, tbl_7, tbl_8, tbl_9, tbl_10, tbl_11, tbl_12, tbl_13, tbl_14, tbl_15, tbl_16, tbl_17, tbl_18, tbl_19, tbl_20, tbl_21, tbl_22, tbl_23, tbl_24, tbl_25, tbl_26, tbl_27, tbl_28, tbl_29, tbl_30, tbl_31, tbl_32, tbl_33, tbl_34, tbl_35, tbl_36, tbl_37, tbl_38, W_top1, b_top1, W_top2, b_top2, W_top3)
    dense_ctx, ids, tbl_0, tbl_1, tbl_2, tbl_3, tbl_4, tbl_5, tbl_6, tbl_7, tbl_8, tbl_9, tbl_10, tbl_11, tbl_12, tbl_13, tbl_14, tbl_15, tbl_16, tbl_17, tbl_18, tbl_19, tbl_20, tbl_21, tbl_22, tbl_23, tbl_24, tbl_25, tbl_26, tbl_27, tbl_28, tbl_29, tbl_30, tbl_31, tbl_32, tbl_33, tbl_34, tbl_35, tbl_36, tbl_37, tbl_38, W_top1, b_top1, W_top2, b_top2, W_top3 = _rec_inputs()

    def _L0_rec_setup():
        import jax, jax.numpy as jnp
        import numpy as np
        B, F0, D = (256, 39, 16)
        CROSS = [128, 128, 128]
        key = jax.random.key(seed)
        k0, k1, k2, k3 = jax.random.split(key, 4)
        inputs = jax.random.normal(k0, (B, F0, D), dtype=jnp.float32)
        f0 = jax.random.normal(k1, (F0 * F0, CROSS[0]), dtype=jnp.float32) * 0.05
        f1 = jax.random.normal(k2, (CROSS[0] * F0, CROSS[1]), dtype=jnp.float32) * 0.05
        f2 = jax.random.normal(k3, (CROSS[1] * F0, CROSS[2]), dtype=jnp.float32) * 0.05
        return {'inputs': inputs, 'f0': f0, 'f1': f1, 'f2': f2}
    _L0_rec_all = _L0_rec_setup()
    _L0_rec_in = {k: v for k, v in _L0_rec_all.items() if k in ('f0', 'f1', 'f2')}
    del _L0_rec_all
    return {'dense_ctx': dense_ctx, 'ids': ids, 'tbl_0': tbl_0, 'tbl_1': tbl_1, 'tbl_2': tbl_2, 'tbl_3': tbl_3, 'tbl_4': tbl_4, 'tbl_5': tbl_5, 'tbl_6': tbl_6, 'tbl_7': tbl_7, 'tbl_8': tbl_8, 'tbl_9': tbl_9, 'tbl_10': tbl_10, 'tbl_11': tbl_11, 'tbl_12': tbl_12, 'tbl_13': tbl_13, 'tbl_14': tbl_14, 'tbl_15': tbl_15, 'tbl_16': tbl_16, 'tbl_17': tbl_17, 'tbl_18': tbl_18, 'tbl_19': tbl_19, 'tbl_20': tbl_20, 'tbl_21': tbl_21, 'tbl_22': tbl_22, 'tbl_23': tbl_23, 'tbl_24': tbl_24, 'tbl_25': tbl_25, 'tbl_26': tbl_26, 'tbl_27': tbl_27, 'tbl_28': tbl_28, 'tbl_29': tbl_29, 'tbl_30': tbl_30, 'tbl_31': tbl_31, 'tbl_32': tbl_32, 'tbl_33': tbl_33, 'tbl_34': tbl_34, 'tbl_35': tbl_35, 'tbl_36': tbl_36, 'tbl_37': tbl_37, 'tbl_38': tbl_38, 'W_top1': W_top1, 'b_top1': b_top1, 'W_top2': W_top2, 'b_top2': b_top2, 'W_top3': W_top3, 'L0_rec_f0': _L0_rec_in['f0'], 'L0_rec_f1': _L0_rec_in['f1'], 'L0_rec_f2': _L0_rec_in['f2']}

def reference(dense_ctx, ids, tbl_0, tbl_1, tbl_2, tbl_3, tbl_4, tbl_5, tbl_6, tbl_7, tbl_8, tbl_9, tbl_10, tbl_11, tbl_12, tbl_13, tbl_14, tbl_15, tbl_16, tbl_17, tbl_18, tbl_19, tbl_20, tbl_21, tbl_22, tbl_23, tbl_24, tbl_25, tbl_26, tbl_27, tbl_28, tbl_29, tbl_30, tbl_31, tbl_32, tbl_33, tbl_34, tbl_35, tbl_36, tbl_37, tbl_38, W_top1, b_top1, W_top2, b_top2, W_top3, L0_rec_f0, L0_rec_f1, L0_rec_f2):
    import jax
    import jax.numpy as jnp

    def _L0_rec_ref(inputs, f0, f1, f2):
        import jax, jax.numpy as jnp
        import numpy as np
        B, F0, D = (256, 39, 16)
        CROSS = [128, 128, 128]
        filters = [f0, f1, f2]
        x0 = inputs
        xk = inputs
        outs = []
        for W in filters:
            b, f, d = x0.shape
            g = xk.shape[1]
            z = jnp.einsum('bfd,bgd->bfgd', x0, xk).reshape(b, f * g, d)
            cur = jnp.einsum('bpd,pm->bmd', z, W)
            outs.append(cur)
            xk = cur
        result = jnp.concatenate(outs, axis=1)
        return jnp.sum(result, axis=-1)
    e = jnp.stack([tbl_0[ids[:, 0]], tbl_1[ids[:, 1]], tbl_2[ids[:, 2]], tbl_3[ids[:, 3]], tbl_4[ids[:, 4]], tbl_5[ids[:, 5]], tbl_6[ids[:, 6]], tbl_7[ids[:, 7]], tbl_8[ids[:, 8]], tbl_9[ids[:, 9]], tbl_10[ids[:, 10]], tbl_11[ids[:, 11]], tbl_12[ids[:, 12]], tbl_13[ids[:, 13]], tbl_14[ids[:, 14]], tbl_15[ids[:, 15]], tbl_16[ids[:, 16]], tbl_17[ids[:, 17]], tbl_18[ids[:, 18]], tbl_19[ids[:, 19]], tbl_20[ids[:, 20]], tbl_21[ids[:, 21]], tbl_22[ids[:, 22]], tbl_23[ids[:, 23]], tbl_24[ids[:, 24]], tbl_25[ids[:, 25]], tbl_26[ids[:, 26]], tbl_27[ids[:, 27]], tbl_28[ids[:, 28]], tbl_29[ids[:, 29]], tbl_30[ids[:, 30]], tbl_31[ids[:, 31]], tbl_32[ids[:, 32]], tbl_33[ids[:, 33]], tbl_34[ids[:, 34]], tbl_35[ids[:, 35]], tbl_36[ids[:, 36]], tbl_37[ids[:, 37]], tbl_38[ids[:, 38]]], axis=1)
    z = _L0_rec_ref(e, L0_rec_f0, L0_rec_f1, L0_rec_f2)
    z = z.reshape(z.shape[0], -1)
    h = jnp.concatenate([z, dense_ctx], axis=1)
    h = jnp.maximum(h @ W_top1 + b_top1, 0.0)
    h = jnp.maximum(h @ W_top2 + b_top2, 0.0)
    y = h @ W_top3
    return y

_drawn_inputs = setup_inputs


def setup_inputs(seed=0):
    import zlib

    import numpy as np

    out = dict(_drawn_inputs(seed))
    spreads = {'b_top1': (0.0, 0.599), 'b_top2': (0.0, 0.28)}
    factors = {'tbl_0': 4.515,
     'tbl_1': 5.243,
     'tbl_2': 4.574,
     'tbl_3': 4.603,
     'tbl_4': 4.798,
     'tbl_5': 5.076,
     'tbl_6': 4.436,
     'tbl_7': 4.767,
     'tbl_8': 5.235,
     'tbl_9': 4.362,
     'tbl_10': 5.098,
     'tbl_11': 4.538,
     'tbl_12': 4.389,
     'tbl_13': 4.455,
     'tbl_14': 4.898,
     'tbl_15': 4.639,
     'tbl_16': 5.266,
     'tbl_17': 5.144,
     'tbl_18': 5.23,
     'tbl_19': 5.447,
     'tbl_20': 5.055,
     'tbl_21': 4.843,
     'tbl_22': 4.649,
     'tbl_23': 4.821,
     'tbl_24': 4.794,
     'tbl_25': 4.652,
     'tbl_26': 4.886,
     'tbl_27': 5.057,
     'tbl_28': 4.917,
     'tbl_29': 4.853,
     'tbl_30': 5.17,
     'tbl_31': 4.585,
     'tbl_32': 4.836,
     'tbl_33': 4.614,
     'tbl_34': 4.977,
     'tbl_35': 4.569,
     'tbl_36': 4.833,
     'tbl_37': 5.114,
     'tbl_38': 5.095,
     'L0_rec_f1': 5.146,
     'L0_rec_f2': 8.0}
    for name, (base, spread) in spreads.items():
        noise = np.random.default_rng([zlib.crc32(name.encode()), seed]).standard_normal(out[name].shape)
        drawn = base * np.exp(spread * noise) if base else spread * noise
        out[name] = jnp.asarray(drawn.astype(out[name].dtype))
    for name, factor in factors.items():
        out[name] = (out[name] * factor).astype(out[name].dtype)
    return out
```

```python
from contextlib import ExitStack

import concourse.bass as bass
from concourse import mybir

ALU = mybir.AluOpType
ACT = mybir.ActivationFunctionType
AX = mybir.AxisListType
F32 = mybir.dt.float32
F32R = mybir.dt.float32r
I32 = mybir.dt.int32
U32 = mybir.dt.uint32

P = 128
NF = 39
D = 16
B = 512
H = 128
B8 = P // D
GT = 4
NG = B // (B8 * GT)
TG = P // (B8 * GT)
NTURN = NG // TG
GROWS = GT * P
LO = 64
KX = LO + NF
KREP = 3
NPAIR = KREP * NF
NJ = 7
NK = (NF + 1) // 2
LASTP = (NK - KREP * (NJ - 1)) * NF
FQ = 4
NQ = (NF + FQ - 1) // FQ
ACT_Q = [0, 2, 4, 5, 7, 9]
DVE_Q = [1, 3, 6, 8]
NSLOT = sum(min(FQ, NF - FQ * q) for q in ACT_Q)
HALF = (NSLOT + 1) // 2
NT = 4
F1 = NF + 1
HID1, HID2 = 512, 256
ND = 16
C_ID, C_MASK, C_SEL = 0, P, P + B8
C_SELX = C_SEL + (NJ + 1) * NPAIR
NC_CONST = C_SELX + F1


def fields(q):
    return range(FQ * q, min(FQ * q + FQ, NF))


def build(nc, ids, tables, consts, w0a, w0b, w1, w2, dense_t, wt1, bt1, wt2, bt2, wt3, out):
    with ExitStack() as ctx:
        def sb(name, shape, dt=F32):
            return ctx.enter_context(nc.sbuf_tensor(name, shape, dt))

        def ps(name, shape):
            return ctx.enter_context(nc.psum_tensor(name, shape, F32))

        def sem(name):
            return ctx.enter_context(nc.semaphore(name))

        t_ps = ps("t_ps", [P, NT, 512])
        b_ps = ps("b_ps", [P, 2, 512])
        cur0_ps = ps("cur0_ps", [P, 512])
        misc_ps = ps("misc_ps", [P, 512])
        s_ps = misc_ps[:, 0:F1 * B8]
        xr_ps = misc_ps[:, F1 * B8:F1 * B8 + GT * F1]

        w1hi = sb("w1hi", [P, NF * H], F32R)
        w1lo = sb("w1lo", [P, NF * H], F32R)
        w2_sb = sb("w2_sb", [P, NF, H])
        s_sb = sb("s_sb", [P, F1, P])
        w1_stage = s_sb[:, 0:NF, :].rearrange("p f m -> p (f m)")
        prod = sb("prod", [P, 2, NSLOT, H])
        stage = prod[:, :, :, :].rearrange("p a s m -> p (a s m)")
        c_stage = stage[:, 0:NC_CONST]
        w0a_st = stage[:, NC_CONST:NC_CONST + NJ * H]
        w0b_st = stage[:, NC_CONST + NJ * H:NC_CONST + 2 * NJ * H]
        ident = sb("ident", [P, P])
        mask = sb("mask", [P, B8])
        sel = sb("sel", [P, NC_CONST - C_SEL], F32R)
        selx = sel[0:KX, C_SELX - C_SEL:C_SELX - C_SEL + F1]
        w0s = sb("w0s", [P, NJ * H])
        idx = sb("idx", [P, NF], I32)
        e_sb = sb("e_sb", [P, NF, D])
        e2 = sb("e2", [P, D, KX])
        xt = sb("xt", [P, TG * GROWS], F32R)
        xs = sb("xs", [P, GROWS], F32R)
        a3 = sb("a3", [P, GROWS])
        z = sb("z", [P, 2, GROWS])
        chi = sb("chi", [P, GROWS], F32R)
        clo = sb("clo", [P, GROWS], F32R)
        xr = sb("xr", [P, GT, F1])
        xbd = sb("xbd", [P, 2, F1, B8])
        cur1 = sb("cur1", [P, 2, H])
        z0t = sb("z0t", [P, B])
        z1t = sb("z1t", [P, B])
        z2t = sb("z2t", [P, B])
        dt_sb = sb("dt_sb", [ND, B])
        wt1_sb = sb("wt1_sb", [P, 3, HID1])
        wt1d_sb = sb("wt1d_sb", [ND, HID1])
        wt2_sb = sb("wt2_sb", [P, HID1 // P, HID2])
        wt3_sb = sb("wt3_sb", [P, HID2 // P])
        b1_sb = sb("b1_sb", [P, HID1 // P])
        b2_sb = sb("b2_sb", [P, HID2 // P])
        h1t = stage[:, 0:HID1 // P * B].rearrange("p (n b) -> p n b", b=B)
        h2t = stage[:, HID1 // P * B:(HID1 + HID2) // P * B].rearrange("p (n b) -> p n b", b=B)
        y_sb = sb("y_sb", [1, B])

        START = 1
        idx_in = sem("idx_in")
        const_in = sem("const_in")
        w0_in = sem("w0_in")
        w1_in = sem("w1_in")
        w2_in = sem("w2_in")
        top_in = sem("top_in")
        gathered = sem("gathered")
        padded = sem("padded")
        consts_done = sem("consts_done")
        w0_added = sem("w0_added")
        w0_done = sem("w0_done")
        w1hi_done = sem("w1hi_done")
        w1lo_done = sem("w1lo_done")
        e2_hi = sem("e2_hi")
        e2_done = sem("e2_done")
        xt_mm = sem("xt_mm")
        xt_done = sem("xt_done")
        xs_done = sem("xs_done")
        a3_mm = sem("a3_mm")
        a3_done = sem("a3_done")
        xr_mm = sem("xr_mm")
        xr_done = sem("xr_done")
        b_mm = sem("b_mm")
        z_done = sem("z_done")
        z_used = sem("z_used")
        chi_done = sem("chi_done")
        clo_done = sem("clo_done")
        summed0 = sem("summed0")
        t_ready = sem("t_ready")
        act_done = sem("act_done")
        dve_done = sem("dve_done")
        halved = sem("halved")
        pool_step = sem("pool_step")
        cur1_done = sem("cur1_done")
        xbd_done = sem("xbd_done")
        s_mm = sem("s_mm")
        s_done = sem("s_done")
        out2_mm = sem("out2_mm")
        out2_done = sem("out2_done")
        h1_mm = sem("h1_mm")
        h1_done = sem("h1_done")
        h2_mm = sem("h2_mm")
        h2_done = sem("h2_done")
        y_mm = sem("y_mm")
        y_done = sem("y_done")
        y_out = sem("y_out")

        block = ctx.enter_context(nc.Block())

        def walk(eng, body):
            with eng.Fori(0, NTURN - 1) as turn:
                with eng.Fori(0, TG - 1) as gi:
                    body(turn, gi, False, False)
                body(turn, TG - 1, True, False)
            with eng.Fori(0, TG - 1) as gi:
                body(NTURN - 1, gi, False, False)
            body(NTURN - 1, TG - 1, False, True)

        @block.sync
        def _(sp):
            sp.dma_start(idx[:, :], ids[0:P, :]).then_inc(idx_in, 16)
            sp.dma_start(c_stage, consts).then_inc(const_in, 16)
            sp.dma_start(w0a_st[0:NPAIR, :].rearrange("p (j m) -> p j m", m=H), w0a).then_inc(w0_in, 16)
            sp.dma_start(w0b_st[0:NPAIR, :].rearrange("p (j m) -> p j m", m=H), w0b).then_inc(w0_in, 16)
            sp.dma_start(w2_sb[:, :, :], w2.rearrange("(f h) m -> h f m", h=H)).then_inc(w2_in, 16)
            sp.dma_start(wt1_sb[:, :, :], wt1[0:3 * P, :].rearrange("(k p) n -> p k n", p=P)).then_inc(top_in, 16)
            sp.dma_start(wt1d_sb[:, :], wt1[3 * P:3 * P + ND, :]).then_inc(top_in, 16)
            sp.dma_start(wt2_sb[:, :, :], wt2.rearrange("(k p) n -> p k n", p=P)).then_inc(top_in, 16)
            sp.dma_start(wt3_sb[:, :], wt3).then_inc(top_in, 16)
            sp.dma_start(b1_sb[:, :], bt1).then_inc(top_in, 16)
            sp.dma_start(b2_sb[:, :], bt2).then_inc(top_in, 16)
            sp.dma_start(dt_sb[:, :], dense_t).then_inc(top_in, 16)
            with sp.Fori(1, NTURN) as turn:
                sp.wait_ge(gathered, turn * (16 * NF))
                sp.dma_start(idx[:, :], ids[bass.ts(turn, P), :]).then_inc(idx_in, 16)
            sp.wait_ge(y_done, 1)
            sp.dma_start(out, y_sb[:, :]).then_inc(y_out, 16)
            sp.wait_ge(y_out, 16)

        @block.gpsimd
        def _(pool):
            def gather(fs):
                for f in fs:
                    nc.gpsimd.indirect_dma_start(
                        out=e_sb[:, f, :], out_offset=None, in_=tables[f],
                        in_offset=bass.IndirectOffsetOnAxis(ap=idx[:, f:f + 1].bitcast(U32), axis=0),
                    ).then_inc(gathered, 16)

            def tile(t, s, xr_count):
                u = s % 2
                v = prod[:, u, :, :]
                pool.wait_ge(xr_done, xr_count)
                if not isinstance(t, int) or t >= 2:
                    pool.wait_ge(s_mm, t + (START - 1))
                nc.gpsimd.tensor_tensor(
                    xbd[:, u, :, :],
                    xr[:, s, :].rearrange("p (f o) -> p f o", o=1).broadcast_to([P, F1, B8]),
                    mask[:, :].rearrange("p (o b) -> p o b", o=1).broadcast_to([P, F1, B8]),
                    ALU.mult).then_inc(xbd_done, 1)
                pool.wait_ge(halved, t + 1)
                nc.gpsimd.tensor_tensor(v[:, 0:6, :], v[:, 0:6, :], v[:, 6:12, :], ALU.add).then_inc(pool_step, 1)
                pool.wait_ge(pool_step, t * 3 + 1)
                nc.gpsimd.tensor_tensor(v[:, 0:3, :], v[:, 0:3, :], v[:, 3:6, :], ALU.add).then_inc(pool_step, 1)
                pool.wait_ge(pool_step, t * 3 + 2)
                nc.gpsimd.tensor_tensor(v[:, 0, :], v[:, 0, :], v[:, 1, :], ALU.add).then_inc(pool_step, 1)
                pool.wait_ge(pool_step, t * 3 + 3)
                nc.gpsimd.tensor_tensor(cur1[:, u, :], v[:, 0, :], v[:, 2, :], ALU.add).then_inc(cur1_done, 1)

            def body(g, last, fs):
                for n in range(1, GT if last else GT + 1):
                    tile(g * GT + n, n % GT, g * 2 + (1, 1, 2, 3)[n - 1])
                    gather(fs[(n - 1) * len(fs) // GT:n * len(fs) // GT])

            pool.sem_inc(cur1_done, START)
            nc.gpsimd.memset(e2[:, :, NF:LO], 0.0).then_inc(padded, 1)
            nc.gpsimd.memset(xr[:, :, NF:F1], 1.0).then_inc(padded, 1)
            pool.wait_ge(idx_in, 16)
            gather(range(NF))
            pool.wait_ge(consts_done, 3)
            pool.wait_ge(padded, 2)
            tile(0, 0, 1)
            with pool.Fori(0, NTURN - 1) as turn:
                pool.wait_ge(e2_done, turn + 1)
                pool.wait_ge(idx_in, turn * 16 + 32)
                for gi in range(TG):
                    body(turn * TG + gi, False, range(NF * gi // 3, NF * (gi + 1) // 3) if gi < 3 else [])
            with pool.Fori(NG - TG, NG - 1) as g:
                body(g, False, [])
            body(NG - 1, True, [])

        @block.scalar
        def _(act):
            def multiply(t, s, k):
                q = ACT_Q[k]
                act.wait_ge(t_ready, t * NQ + (q + 1))
                bank = (s * NQ + q) % NT
                for i, f in enumerate(fields(q)):
                    ins = nc.scalar.activation(prod[:, s % 2, FQ * k + i, :], t_ps[:, bank, i * H:(i + 1) * H],
                                               ACT.Copy, scale=xr[:, s, f:f + 1])
                ins.then_inc(act_done, 1)

            def xt_out(turn, ns):
                for n in ns:
                    act.wait_ge(xt_mm, turn * 4 + (n + 1))
                    nc.scalar.activation(
                        xt[0:KX, :].rearrange("p (t d b) -> p d t b", d=D, b=B8)[:, 4 * n:4 * n + 4],
                        b_ps[0:KX, n % 2, :].rearrange("p (d t b) -> p d t b", d=4, b=B8),
                        ACT.Copy).then_inc(xt_done, 1)

            def xs_copy(g, gi, turn):
                if not isinstance(g, int) or g > 0:
                    act.wait_ge(b_mm, g * NJ)
                act.wait_ge(xt_done, turn * 4 + 4)
                src = xt[0:KX, bass.ts(gi, GROWS)]
                nc.scalar.activation(xs[0:KX, :], src, ACT.Copy).then_inc(xs_done, 1)

            def a3_out(g):
                act.wait_ge(a3_mm, g + 1)
                nc.scalar.activation(a3[0:NPAIR, :], b_ps[0:NPAIR, 0, :], ACT.Copy).then_inc(a3_done, 1)

            def xr_out(g, lo, hi):
                act.wait_ge(xr_mm, g + 1)
                if not isinstance(g, int) or g > 0:
                    act.wait_ge(dve_done, g * (GT * len(DVE_Q)) - (GT - hi) * len(DVE_Q))
                    act.wait_ge(xbd_done, g * GT - (GT - hi))
                nc.scalar.activation(xr[:, lo:hi, 0:NF],
                                     xr_ps.rearrange("p (t f) -> p t f", f=F1)[:, lo:hi, 0:NF],
                                     ACT.Copy).then_inc(xr_done, 1)

            def chi_out(g, lo, hi):
                act.wait_ge(z_used, g * NJ + NJ)
                if hi == GT:
                    act.wait_ge(summed0, g + 1)
                if not isinstance(g, int) or g > 0:
                    act.wait_ge(t_ready, g * (GT * NQ) - (GT - hi) * NQ)
                nc.scalar.activation(chi[:, lo * P:hi * P], cur0_ps[:, lo * P:hi * P],
                                     ACT.Copy).then_inc(chi_done, 1)

            def s_out(t, col):
                act.wait_ge(s_mm, t + (START + 1))
                nc.scalar.activation(s_sb[:, :, bass.ds(col, B8)],
                                     s_ps.rearrange("p (f b) -> p f b", b=B8), ACT.Copy).then_inc(s_done, 1)

            def out2_out(turn):
                act.wait_ge(out2_mm, turn + 1)
                nc.scalar.activation(z2t[:, bass.ts(turn, P)], cur0_ps[:, 0:P], ACT.Copy)
                nc.scalar.activation(z1t[:, bass.ts(turn, P)], s_sb[:, NF, :], ACT.Copy).then_inc(out2_done, 1)

            def body(turn, gi, turns, last):
                g = turn * TG + gi
                for n in range(1, GT if last else GT + 1):
                    t, s = g * GT + n, n % GT
                    act.wait_ge(cur1_done, t + (START - 1))
                    for k in range(len(ACT_Q)):
                        multiply(t, s, k)
                        if last:
                            pass
                        elif n == 1 and k in (2, 3) and turns:
                            xt_out(turn + 1, (2 * k - 4, 2 * k - 3))
                            if k == 3:
                                xs_copy(g + 1, 0, turn + 1)
                        elif n == 1 and k == 2:
                            xs_copy(g + 1, gi + 1, turn)
                        elif n == 1 and k == 4:
                            a3_out(g + 1)
                        elif n == 3 and k == 3:
                            xr_out(g + 1, 0, GT - 1)
                        elif n == 3 and k == 4:
                            chi_out(g + 1, 0, GT - 1)
                        elif n == 4 and k == 1:
                            chi_out(g + 1, GT - 1, GT)
                        elif n == 4 and k == 3:
                            xr_out(g + 1, GT - 1, GT)
                    s_out(t - 1, gi * (GT * B8) + (n - 1) * B8)
                if turns:
                    out2_out(turn)

            act.sem_inc(s_done, START)
            act.dma_start(w1_stage.rearrange("p (f m) -> p f m", m=H),
                          w1.rearrange("(f h) m -> h f m", h=H)).then_inc(w1_in, 16)
            act.wait_ge(w1_in, 16)
            nc.scalar.activation(w1hi[:, :], w1_stage, ACT.Copy).then_inc(w1hi_done, 1)
            xt_out(0, range(D // 4))
            xs_copy(0, 0, 0)
            a3_out(0)
            xr_out(0, 0, GT - 1)
            xr_out(0, GT - 1, GT)
            chi_out(0, 0, GT - 1)
            chi_out(0, GT - 1, GT)
            act.wait_ge(consts_done, 3)
            act.wait_ge(w0_done, 1)
            for k in range(len(ACT_Q)):
                multiply(0, 0, k)
            walk(act, body)
            s_out(NG * GT - 1, (TG * GT - 1) * B8)
            out2_out(NTURN - 1)
            for n in range(HID1 // P):
                act.wait_ge(h1_mm, n + 1)
                nc.scalar.activation(h1t[:, n, :], t_ps[:, n, :], ACT.Relu, bias=b1_sb[:, n:n + 1]).then_inc(h1_done, 1)
            for n in range(HID2 // P):
                act.wait_ge(h2_mm, n + 1)
                nc.scalar.activation(h2t[:, n, :], b_ps[:, n, :], ACT.Relu, bias=b2_sb[:, n:n + 1]).then_inc(h2_done, 1)
            act.wait_ge(y_mm, 1)
            nc.scalar.activation(y_sb[:, :], misc_ps[0:1, :], ACT.Copy).then_inc(y_done, 1)

        @block.vector
        def _(dve):
            def split_e(turn):
                dve.wait_ge(gathered, turn * (16 * NF) + 16 * NF)
                if not isinstance(turn, int) or turn > 0:
                    dve.wait_ge(xt_mm, turn * 4)
                src = e_sb[:, :, :].rearrange("p f d -> p d f")
                nc.vector.tensor_copy(e2[:, :, 0:NF].bitcast(F32R), src).then_inc(e2_hi, 1)
                dve.wait_ge(e2_hi, turn + 1)
                nc.vector.tensor_tensor(e2[:, :, LO:KX], src, e2[:, :, 0:NF], ALU.subtract).then_inc(e2_done, 1)

            def pair_product(g, j):
                dve.wait_ge(b_mm, g * NJ + (j + 1))
                if j == 0:
                    dve.wait_ge(a3_done, g + 1)
                if not isinstance(g, int) or g > 0 or j >= 2:
                    dve.wait_ge(z_used, g * NJ + max(j - 1, 0))
                n = NPAIR if j < NJ - 1 else LASTP
                nc.vector.tensor_tensor(z[0:n, j % 2, :], b_ps[0:n, (j + 1) % 2, :], a3[0:n, :],
                                        ALU.mult).then_inc(z_done, 1)

            def clo_out(g, lo, hi):
                dve.wait_ge(chi_done, g * 2 + (1 if hi < GT else 2))
                c = slice(lo * P, hi * P)
                nc.vector.tensor_tensor(clo[:, c], cur0_ps[:, c], chi[:, c].bitcast(F32),
                                        ALU.subtract).then_inc(clo_done, 1)

            def sum_cur0(g):
                dve.wait_ge(z_used, g * NJ + NJ)
                nc.vector.tensor_reduce(z0t[:, bass.ts(g, GT * B8)].rearrange("p (t b) -> p t b", b=B8),
                                        cur0_ps[:, :].rearrange("p (t d b) -> p t b d", d=D, b=B8),
                                        AX.X, ALU.add).then_inc(summed0, 1)

            def fused(t, s, k):
                q = DVE_Q[k]
                dve.wait_ge(t_ready, t * NQ + (q + 1))
                dve.wait_ge(act_done, t * len(ACT_Q) + (k + 1))
                bank = (s * NQ + q) % NT
                for i, f in enumerate(fields(q)):
                    v = prod[:, s % 2, FQ * k + i, :]
                    ins = nc.vector.scalar_tensor_tensor(out=v, in0=t_ps[:, bank, i * H:(i + 1) * H],
                                                         scalar=xr[:, s, f:f + 1], in1=v,
                                                         op0=ALU.mult, op1=ALU.add)
                ins.then_inc(dve_done, 1)

            def halve(t, s):
                dve.wait_ge(act_done, t * len(ACT_Q) + len(ACT_Q))
                dve.wait_ge(dve_done, t * len(DVE_Q) + len(DVE_Q))
                v = prod[:, s % 2, :, :]
                n = NSLOT - HALF
                nc.vector.tensor_tensor(v[:, 0:n, :], v[:, 0:n, :], v[:, HALF:NSLOT, :], ALU.add).then_inc(halved, 1)

            def body(turn, gi, turns, last):
                g = turn * TG + gi
                for n in range(1, GT if last else GT + 1):
                    t, s = g * GT + n, n % GT
                    if n == 1 and turns:
                        split_e(turn + 1)
                    for k in range(len(DVE_Q)):
                        fused(t, s, k)
                        if last:
                            pass
                        elif n == 1 and k == 3:
                            pair_product(g + 1, 0)
                        elif n == 2:
                            pair_product(g + 1, 1 + k)
                        elif n == 3 and k < 2:
                            pair_product(g + 1, 5 + k)
                        elif n == 3 and k == 3:
                            clo_out(g + 1, 0, GT - 1)
                        elif n == 4 and k == 1:
                            clo_out(g + 1, GT - 1, GT)
                    halve(t, s)
                    if n == 3 and not last:
                        sum_cur0(g + 1)

            dve.wait_ge(const_in, 16)
            nc.vector.tensor_copy(ident[:, :], c_stage[:, C_ID:C_ID + P]).then_inc(consts_done, 1)
            nc.vector.tensor_copy(mask[:, :], c_stage[:, C_MASK:C_MASK + B8]).then_inc(consts_done, 1)
            nc.vector.tensor_copy(sel[:, :], c_stage[:, C_SEL:NC_CONST]).then_inc(consts_done, 1)
            dve.wait_ge(w0_in, 32)
            nc.vector.tensor_tensor(w0s[0:NPAIR, :], w0a_st[0:NPAIR, :], w0b_st[0:NPAIR, :], ALU.add).then_inc(w0_added, 1)
            dve.wait_ge(w0_added, 1)
            nc.vector.tensor_copy(w0s[0:NF, 0:H], w0a_st[0:NF, 0:H]).then_inc(w0_done, 1)
            dve.wait_ge(w1hi_done, 1)
            nc.vector.tensor_tensor(w1lo[:, :], w1_stage, w1hi[:, :].bitcast(F32), ALU.subtract).then_inc(w1lo_done, 1)
            split_e(0)
            for j in range(NJ):
                pair_product(0, j)
            clo_out(0, 0, GT - 1)
            sum_cur0(0)
            clo_out(0, GT - 1, GT)
            for k in range(len(DVE_Q)):
                fused(0, 0, k)
            halve(0, 0)
            walk(dve, body)

        @block.tensor
        def _(pe):
            def transposes(turn, n):
                if n == 0:
                    pe.wait_ge(e2_done, turn + 1)
                    if not isinstance(turn, int) or turn > 0:
                        pe.wait_ge(z_done, turn * (TG * NJ))
                if n >= 2:
                    pe.wait_ge(xt_done, turn * 4 + (n - 1))
                for i in range(4):
                    ins = nc.tensor.transpose(b_ps[0:KX, n % 2, i * P:(i + 1) * P], e2[:, 4 * n + i, :], ident[:, :])
                ins.then_inc(xt_mm, 1)

            def spread_a(g):
                pe.wait_ge(xs_done, g + 1)
                if not isinstance(g, int) or g > 0:
                    pe.wait_ge(z_done, g * NJ)
                nc.tensor.matmul(b_ps[0:NPAIR, 0, :], sel[0:KX, 0:NPAIR], xs[0:KX, :],
                                 start=True, stop=True).then_inc(a3_mm, 1)

            def row_major(g):
                if not isinstance(g, int) or g > 0:
                    pe.wait_ge(xr_done, g * 2)
                    pe.wait_ge(s_done, g * GT - (GT - 1) + START)
                for i in range(GT):
                    ins = nc.tensor.matmul(xr_ps[:, i * F1:(i + 1) * F1], xs[0:KX, i * P:(i + 1) * P], selx,
                                           start=True, stop=True, skip_group_check=True)
                ins.then_inc(xr_mm, 1)

            def spread_b(g, j):
                if j == 1:
                    pe.wait_ge(a3_done, g + 1)
                if j >= 2:
                    pe.wait_ge(z_done, g * NJ + (j - 1))
                c = (1 + j) * NPAIR
                nc.tensor.matmul(b_ps[0:NPAIR, (j + 1) % 2, :], sel[0:KX, c:c + NPAIR], xs[0:KX, :],
                                 start=True, stop=True).then_inc(b_mm, 1)

            def contract0(g, j):
                if j == 0 and (not isinstance(g, int) or g > 0):
                    pe.wait_ge(clo_done, g * 2)
                pe.wait_ge(z_done, g * NJ + (j + 1))
                n = NPAIR if j < NJ - 1 else LASTP
                nc.tensor.matmul(cur0_ps[:, :], w0s[0:n, j * H:(j + 1) * H], z[0:n, j % 2, :],
                                 start=(j == 0), stop=(j == NJ - 1)).then_inc(z_used, 1)

            def free_bank(t, q):
                q, t = (q - NT, t) if q >= NT else (q - NT + NQ, t - 1)
                if isinstance(t, int) and t < 0:
                    return
                if q in ACT_Q:
                    pe.wait_ge(act_done, t * len(ACT_Q) + (ACT_Q.index(q) + 1))
                else:
                    pe.wait_ge(dve_done, t * len(DVE_Q) + (DVE_Q.index(q) + 1))

            def contract1(t, s, q):
                free_bank(t, q)
                c = slice(s * P, (s + 1) * P)
                w = slice(FQ * q * H, (fields(q)[-1] + 1) * H)
                o = t_ps[:, (s * NQ + q) % NT, 0:w.stop - w.start]
                nc.tensor.matmul(o, chi[:, c], w1hi[:, w], start=True, stop=False)
                nc.tensor.matmul(o, chi[:, c], w1lo[:, w], start=False, stop=False)
                nc.tensor.matmul(o, clo[:, c], w1hi[:, w], start=False, stop=True).then_inc(t_ready, 1)

            def contract_d(t, s):
                u = s % 2
                pe.wait_ge(cur1_done, t + (START + 1))
                pe.wait_ge(xbd_done, t + 1)
                pe.wait_ge(s_done, t + START)
                nc.tensor.matmul(s_ps, cur1[:, u, :], xbd[:, u, :, :].rearrange("p f b -> p (f b)"),
                                 start=True, stop=True, skip_group_check=True).then_inc(s_mm, 1)

            def layer2(g):
                pe.wait_ge(s_done, g * GT + (GT + START))
                for f in range(NF):
                    ins = nc.tensor.matmul(cur0_ps[:, 0:P], w2_sb[:, f, :], s_sb[:, f, :],
                                           start=(f == 0), stop=(f == NF - 1))
                ins.then_inc(out2_mm, 1)

            def body(turn, gi, turns, last):
                g = turn * TG + gi
                for n in range(1, GT if last else GT + 1):
                    t, s = g * GT + n, n % GT
                    if n == 3:
                        pe.wait_ge(clo_done, g * 2 + 2)
                    if n == 4:
                        pe.wait_ge(clo_done, g * 2 + 3)
                    for q in range(NQ):
                        contract1(t, s, q)
                        if q == 8:
                            if n >= 3 and not last:
                                pe.wait_ge(xr_done, g * 2 + n)
                            contract_d(t - 1, (n - 1) % GT)
                        if last:
                            continue
                        if n == 1:
                            if turns and q in (2, 3, 4, 5):
                                transposes(turn + 1, q - 2)
                            if q == 6:
                                spread_a(g + 1)
                            if q in (8, 9):
                                spread_b(g + 1, q - 8)
                        if (n, q) == (2, 4):
                            row_major(g + 1)
                        at = [(2, 0), (2, 3), (2, 5), (2, 8), (3, 0), (3, 3), (3, 5)]
                        if (n, q) in at:
                            j = at.index((n, q))
                            contract0(g + 1, j)
                            if j + 2 < NJ:
                                spread_b(g + 1, j + 2)
                if turns:
                    pe.wait_ge(clo_done, g * 2 + 4)
                    layer2(g)

            pe.sem_inc(s_mm, START)
            pe.wait_ge(consts_done, 3)
            pe.wait_ge(padded, 2)
            for n in range(D // 4):
                transposes(0, n)
            spread_a(0)
            row_major(0)
            spread_b(0, 0)
            spread_b(0, 1)
            pe.wait_ge(w0_done, 1)
            for j in range(NJ):
                contract0(0, j)
                if j + 2 < NJ:
                    spread_b(0, j + 2)
            pe.wait_ge(clo_done, 1)
            pe.wait_ge(w1lo_done, 1)
            for q in range(NQ):
                contract1(0, 0, q)
            pe.wait_ge(w2_in, 16)
            walk(pe, body)
            contract_d(NG * GT - 1, GT - 1)
            layer2(NG - 1)
            pe.wait_ge(top_in, 7 * 16)
            pe.wait_ge(out2_done, NTURN)
            for n in range(HID1 // P):
                c = slice(n * P, (n + 1) * P)
                for k, x in enumerate((z0t, z1t, z2t)):
                    nc.tensor.matmul(t_ps[:, n, :], wt1_sb[:, k, c], x[:, :], start=(k == 0), stop=False)
                nc.tensor.matmul(t_ps[:, n, :], wt1d_sb[:, c], dt_sb[:, :], start=False, stop=True).then_inc(h1_mm, 1)
            for n in range(HID2 // P):
                for k in range(HID1 // P):
                    if n == 0:
                        pe.wait_ge(h1_done, k + 1)
                    ins = nc.tensor.matmul(b_ps[:, n, :], wt2_sb[:, k, n * P:(n + 1) * P], h1t[:, k, :],
                                           start=(k == 0), stop=(k == HID1 // P - 1))
                ins.then_inc(h2_mm, 1)
            for k in range(HID2 // P):
                pe.wait_ge(h2_done, k + 1)
                ins = nc.tensor.matmul(misc_ps[0:1, :], wt3_sb[:, k:k + 1], h2t[:, k, :],
                                       start=(k == 0), stop=(k == HID2 // P - 1))
            ins.then_inc(y_mm, 1)


def _constants():
    import numpy as np
    c = np.zeros((P, NC_CONST), np.float32)
    c[:, C_ID:C_ID + P] = np.eye(P)
    for row in range(P):
        c[row, C_MASK + row % B8] = 1.0
    for p in range(NPAIR):
        f = p % NF
        for r in (f, LO + f):
            c[r, C_SEL + p] = 1.0
        for j in range(NJ):
            g = (f + KREP * j + p // NF) % NF
            for r in (g, LO + g):
                c[r, C_SEL + (1 + j) * NPAIR + p] = 1.0
    for f in range(NF):
        for r in (f, LO + f):
            c[r, C_SELX + f] = 1.0
    return c


def kernel(**inputs):
    import numpy as np
    import concourse.bacc as bacc
    from concourse.bass_utils import run_bass_kernel_spmd

    f0 = np.asarray(inputs["L0_rec_f0"])
    w0a = np.zeros((NPAIR, NJ, H), f0.dtype)
    w0b = np.zeros((NPAIR, NJ, H), f0.dtype)
    for j in range(NJ):
        for kk in range(KREP):
            k = KREP * j + kk
            if k < NK:
                f = np.arange(NF)
                g = (f + k) % NF
                w0a[kk * NF:(kk + 1) * NF, j] = f0[f * NF + g]
                w0b[kk * NF:(kk + 1) * NF, j] = f0[g * NF + f]

    nc = bacc.Bacc("TRN2", target_bir_lowering=False, num_devices=1)
    arrays = {}

    def dram(name, a):
        a = np.ascontiguousarray(a)
        arrays[name] = a
        return nc.dram_tensor(name, a.shape, mybir.dt.from_np(a.dtype), kind="ExternalInput").ap()

    def by_partition(a):
        return np.asarray(a).reshape(-1, P).T

    args = [
        dram("ids", inputs["ids"]),
        [dram(f"tbl_{f}", inputs[f"tbl_{f}"]) for f in range(NF)],
        dram("consts", _constants()),
        dram("w0a", w0a), dram("w0b", w0b),
        dram("w1", inputs["L0_rec_f1"]), dram("w2", inputs["L0_rec_f2"]),
        dram("dense_t", np.asarray(inputs["dense_ctx"]).T),
        dram("w_top1", inputs["W_top1"]), dram("b_top1", by_partition(inputs["b_top1"])),
        dram("w_top2", inputs["W_top2"]), dram("b_top2", by_partition(inputs["b_top2"])),
        dram("w_top3", by_partition(inputs["W_top3"])),
        nc.dram_tensor("y", (1, B), F32, kind="ExternalOutput").ap(),
    ]
    build(nc, *args)
    return run_bass_kernel_spmd(nc, [arrays], core_ids=[0]).results[0]["y"].reshape(B, 1)
```

```python
from contextlib import ExitStack

import concourse.bass as bass
from concourse import mybir

ALU = mybir.AluOpType
ACT = mybir.ActivationFunctionType
AX = mybir.AxisListType
F32 = mybir.dt.float32
F32R = mybir.dt.float32r
I32 = mybir.dt.int32
U32 = mybir.dt.uint32

P = 128
NF = 39
D = 16
B = 512
H = 128
B8 = P // D
GT = 4
NG = B // (B8 * GT)
TG = P // (B8 * GT)
NTURN = NG // TG
GROWS = GT * P
LO = 64
KX = LO + NF
KREP = 3
NPAIR = KREP * NF
NJ = 7
NK = (NF + 1) // 2
LASTP = (NK - KREP * (NJ - 1)) * NF
FQ = 4
NQ = (NF + FQ - 1) // FQ
ACT_Q = [0, 2, 4, 5, 7, 9]
DVE_Q = [1, 3, 6, 8]
NZ = 4
TRANSPOSE_AT = ([], [5, 5, 5, 6])
SPREAD_A_AT = (3, 8)
ROW_MAJOR_AT = (17, 16)
SPREAD_AT = ([4, 4, 6, 6, 11, 17, 24], [8, 11, 13, 14, 15, 20, 23])
CONTRACT_AT = ([11, 11, 13, 13, 22, 25, 26], [12, 17, 20, 21, 24, 25, 26])
PRODUCT_AFTER = ([1, 1, 2, 2, 4, 7, 9], [3, 4, 5, 6, 6, 6, 8])
XT_OUT_AFTER = (2, 3)
XS_AFTER = (0, 3)
A3_OUT_AFTER = (1, 4)
XR_STAGE_AFTER = (11, 8)
XR_OUT_AFTER = (13, 22)
CHI_AFTER = (16, 20)
CLO_AFTER = (11, 13)
SUM_AFTER = 12
GATHER_TILES = 10
NSLOT = sum(min(FQ, NF - FQ * q) for q in ACT_Q)
HALF = (NSLOT + 1) // 2
NR = 7
F1 = NF + 1
HID1, HID2 = 512, 256
ND = 16
C_ID, C_MASK, C_SEL = 0, P, P + B8
C_SELX = C_SEL + (NJ + 1) * NPAIR
NC_CONST = C_SELX + F1


SKIP_AT = ([("T", 1, 8), ("T", 1, 3), ("T", 3, 6)], [])


def fields(q):
    return range(FQ * q, min(FQ * q + FQ, NF))


def plan(turns, last=False):
    steps = []
    for n in range(1, GT if last else GT + 1):
        for q in range(NQ):
            steps.append(("T", n, q))
            if q == NQ - 2:
                steps.append(("S", n))
            at = (n - 1) * NQ + q
            if last:
                continue
            steps += [("X", i) for i, x in enumerate(TRANSPOSE_AT[turns]) if x == at]
            steps += [("A",)] * (SPREAD_A_AT[turns] == at)
            steps += [("C", j) for j, x in enumerate(CONTRACT_AT[turns]) if x == at]
            steps += [("B", j) for j, x in enumerate(SPREAD_AT[turns]) if x == at]
            steps += [("R",)] * (ROW_MAJOR_AT[turns] == at)
    ring = [x for x in steps if x[0] != "C" and x != ("X", 3)]
    place, at = {}, 0
    for x in ring:
        at += (x in SKIP_AT[turns] and not last)
        place[x] = at
        at += 1
    assert last or at % NR == 0, at
    return steps, place


PLANS = [plan(0), plan(1), plan(0, True)]
TAIL = {k: v - (max(PLANS[0][1].values()) + 1) for k, v in PLANS[0][1].items()}
TAIL = {k: v for k, v in TAIL.items() if k[0] in "TS" and k[1] == GT}


def build(nc, ids, tables, consts, w0a, w0b, w1, w2, dense_t, wt1, bt1, wt2, bt2, wt3, out):
    with ExitStack() as ctx:
        def sb(name, shape, dt=F32):
            return ctx.enter_context(nc.sbuf_tensor(name, shape, dt))

        def ps(name, shape):
            return ctx.enter_context(nc.psum_tensor(name, shape, F32))

        def sem(name):
            return ctx.enter_context(nc.semaphore(name))

        ring = ps("ring", [P, NR, 512])
        cur0_ps = ps("cur0_ps", [P, 512])

        w1hi = sb("w1hi", [P, NF * H], F32R)
        w2_sb = sb("w2_sb", [P, NF, H])
        s_sb = sb("s_sb", [P, F1, B - P])
        w1_stage = s_sb[:, :, :].rearrange("p f b -> p (f b)")[:, 0:NF * H]
        prod = sb("prod", [P, 2, NSLOT, H])
        stage = prod[:, :, :, :].rearrange("p a s m -> p (a s m)")
        c_stage = stage[:, 0:NC_CONST]
        w0a_st = stage[:, NC_CONST:NC_CONST + NJ * H]
        w0b_st = stage[:, NC_CONST + NJ * H:NC_CONST + 2 * NJ * H]
        ident = sb("ident", [P, P])
        mask = sb("mask", [P, B8])
        sel = sb("sel", [P, NC_CONST - C_SEL], F32R)
        selx = sel[0:KX, C_SELX - C_SEL:C_SELX - C_SEL + F1]
        w0s = sb("w0s", [P, NJ * H])
        idx = sb("idx", [P, NF], I32)
        e_sb = sb("e_sb", [P, NF, D])
        e2 = sb("e2", [P, D, KX])
        xt = sb("xt", [P, TG * GROWS], F32R)
        xs = sb("xs", [P, GROWS], F32R)
        a3 = sb("a3", [P, GROWS])
        z = sb("z", [P, NZ, GROWS])
        chi = sb("chi", [P, GROWS], F32R)
        clo = sb("clo", [P, GROWS], F32R)
        xr = sb("xr", [P, GT, F1])
        xr_next = sb("xr_next", [P, GT, F1])
        xbd = sb("xbd", [P, 2, F1, B8])
        cur1 = sb("cur1", [P, 2, H])
        z0t = sb("z0t", [P, B])
        z12t = e2[:, :, :].rearrange("p d k -> p (d k)")
        z1t = z12t[:, 0:B]
        z2t = z12t[:, B:2 * B]
        wt3_sb = sb("wt3_sb", [P, HID2 // P])
        b1_sb = sb("b1_sb", [P, HID1 // P])
        b2_sb = sb("b2_sb", [P, HID2 // P])
        h1t = stage[:, 0:HID1 // P * B].rearrange("p (n b) -> p n b", b=B)
        h2t = stage[:, HID1 // P * B:(HID1 + HID2) // P * B].rearrange("p (n b) -> p n b", b=B)
        y_sb = a3[0:1, :]
        w1lo = sb("w1lo", [P, NF * H], F32R)
        wt1_sb = z[:, :, :].rearrange("p a b -> p (a b)")[:, 0:3 * HID1].rearrange("p (k n) -> p k n", n=HID1)
        wt1d_sb = z[0:ND, NZ - 1, 0:HID1]
        wt2_sb = xt[:, 0:HID1 // P * HID2].bitcast(F32).rearrange("p (k n) -> p k n", n=HID2)
        dt_sb = xt[0:ND, HID1 // P * HID2:HID1 // P * HID2 + B].bitcast(F32)

        START = 1
        idx_in = sem("idx_in")
        const_in = sem("const_in")
        w0_in = sem("w0_in")
        w1_in = sem("w1_in")
        w2_in = sem("w2_in")
        top_in = sem("top_in")
        gathered = sem("gathered")
        padded = sem("padded")
        consts_done = sem("consts_done")
        w0_added = sem("w0_added")
        w0_done = sem("w0_done")
        w1hi_done = sem("w1hi_done")
        w1lo_done = sem("w1lo_done")
        e2_hi = sem("e2_hi")
        e2_done = sem("e2_done")
        xt_mm = sem("xt_mm")
        xt_done = sem("xt_done")
        xs_done = sem("xs_done")
        a3_mm = sem("a3_mm")
        a3_done = sem("a3_done")
        xr_mm = sem("xr_mm")
        xrn_done = sem("xrn_done")
        xr_done = sem("xr_done")
        b_mm = sem("b_mm")
        z_done = sem("z_done")
        z_used = sem("z_used")
        chi_done = sem("chi_done")
        clo_done = sem("clo_done")
        summed0 = sem("summed0")
        t_ready = sem("t_ready")
        act_done = sem("act_done")
        dve_done = sem("dve_done")
        halved = sem("halved")
        pool_step = sem("pool_step")
        cur1_done = sem("cur1_done")
        xbd_done = sem("xbd_done")
        s_mm = sem("s_mm")
        s_done = sem("s_done")
        out2_mm = sem("out2_mm")
        z1_done = sem("z1_done")
        out2_done = sem("out2_done")
        h1_mm = sem("h1_mm")
        h1_done = sem("h1_done")
        h2_mm = sem("h2_mm")
        h2_done = sem("h2_done")
        y_mm = sem("y_mm")
        y_done = sem("y_done")
        y_out = sem("y_out")

        block = ctx.enter_context(nc.Block())

        def bank(x, turns, last=False):
            return PLANS[2 if last else int(turns)][1][x] % NR

        def walk(eng, body, before_last=None):
            with eng.Fori(0, NTURN - 1) as turn:
                with eng.Fori(0, TG - 1) as gi:
                    body(turn, gi, False, False)
                body(turn, TG - 1, True, False)
            if before_last:
                before_last()
            with eng.Fori(0, TG - 1) as gi:
                body(NTURN - 1, gi, False, False)
            body(NTURN - 1, TG - 1, False, True)

        @block.sync
        def _(sp):
            sp.dma_start(idx[:, :], ids[0:P, :]).then_inc(idx_in, 16)
            sp.dma_start(c_stage, consts).then_inc(const_in, 16)
            sp.dma_start(w0a_st[0:NPAIR, :].rearrange("p (j m) -> p j m", m=H), w0a).then_inc(w0_in, 16)
            sp.dma_start(w0b_st[0:NPAIR, :].rearrange("p (j m) -> p j m", m=H), w0b).then_inc(w0_in, 16)
            sp.dma_start(w2_sb[:, :, :], w2.rearrange("(f h) m -> h f m", h=H)).then_inc(w2_in, 16)
            sp.dma_start(wt3_sb[:, :], wt3).then_inc(top_in, 16)
            sp.dma_start(b1_sb[:, :], bt1).then_inc(top_in, 16)
            sp.dma_start(b2_sb[:, :], bt2).then_inc(top_in, 16)
            with sp.Fori(1, NTURN) as turn:
                sp.wait_ge(gathered, turn * (16 * NF))
                sp.dma_start(idx[:, :], ids[bass.ts(turn, P), :]).then_inc(idx_in, 16)
            sp.wait_ge(z_used, NG * NJ)
            sp.wait_ge(xs_done, NG)
            sp.dma_start(wt1_sb[:, :, :], wt1[0:3 * P, :].rearrange("(k p) n -> p k n", p=P)).then_inc(top_in, 16)
            sp.dma_start(wt1d_sb, wt1[3 * P:3 * P + ND, :]).then_inc(top_in, 16)
            sp.dma_start(dt_sb, dense_t).then_inc(top_in, 16)
            sp.dma_start(wt2_sb[:, :, :], wt2.rearrange("(k p) n -> p k n", p=P)).then_inc(top_in, 16)
            sp.wait_ge(y_done, 1)
            sp.dma_start(out, y_sb).then_inc(y_out, 16)
            sp.wait_ge(y_out, 16)

        @block.gpsimd
        def _(pool):
            def gather(fs):
                for f in fs:
                    nc.gpsimd.indirect_dma_start(
                        out=e_sb[:, f, :], out_offset=None, in_=tables[f],
                        in_offset=bass.IndirectOffsetOnAxis(ap=idx[:, f:f + 1].bitcast(U32), axis=0),
                    ).then_inc(gathered, 16)

            def tile(t, s, xr_count):
                u = s % 2
                v = prod[:, u, :, :]
                pool.wait_ge(xr_done, xr_count)
                if not isinstance(t, int) or t >= 2:
                    pool.wait_ge(s_mm, t + (START - 1))
                nc.gpsimd.tensor_tensor(
                    xbd[:, u, :, :],
                    xr[:, s, :].rearrange("p (f o) -> p f o", o=1).broadcast_to([P, F1, B8]),
                    mask[:, :].rearrange("p (o b) -> p o b", o=1).broadcast_to([P, F1, B8]),
                    ALU.mult).then_inc(xbd_done, 1)
                pool.wait_ge(halved, t + 1)
                nc.gpsimd.tensor_tensor(v[:, 0:6, :], v[:, 0:6, :], v[:, 6:12, :], ALU.add).then_inc(pool_step, 1)
                pool.wait_ge(pool_step, t * 3 + 1)
                nc.gpsimd.tensor_tensor(v[:, 0:3, :], v[:, 0:3, :], v[:, 3:6, :], ALU.add).then_inc(pool_step, 1)
                pool.wait_ge(pool_step, t * 3 + 2)
                nc.gpsimd.tensor_tensor(v[:, 0, :], v[:, 0, :], v[:, 1, :], ALU.add).then_inc(pool_step, 1)
                pool.wait_ge(pool_step, t * 3 + 3)
                nc.gpsimd.tensor_tensor(cur1[:, u, :], v[:, 0, :], v[:, 2, :], ALU.add).then_inc(cur1_done, 1)

            def body(g, last, gi=TG):
                for n in range(1, GT if last else GT + 1):
                    tile(g * GT + n, n % GT, g * 2 + (1, 1, 2, 3)[n - 1])
                    i = gi * GT + n - 1
                    gather(range(NF * i // GATHER_TILES, min(NF * (i + 1) // GATHER_TILES, NF)))

            pool.sem_inc(cur1_done, START)
            nc.gpsimd.memset(e2[:, :, NF:LO], 0.0).then_inc(padded, 1)
            nc.gpsimd.memset(xr[:, :, NF:F1], 1.0).then_inc(padded, 1)
            pool.wait_ge(idx_in, 16)
            gather(range(NF))
            pool.wait_ge(consts_done, 3)
            pool.wait_ge(padded, 2)
            tile(0, 0, 1)
            with pool.Fori(0, NTURN - 1) as turn:
                pool.wait_ge(e2_done, turn + 1)
                pool.wait_ge(idx_in, turn * 16 + 32)
                for gi in range(TG):
                    body(turn * TG + gi, False, gi)
            with pool.Fori(NG - TG, NG - 1) as g:
                body(g, False)
            body(NG - 1, True)

        @block.scalar
        def _(act):
            def multiply(t, s, k, b):
                q = ACT_Q[k]
                act.wait_ge(t_ready, t * NQ + (q + 1))
                for i, f in enumerate(fields(q)):
                    ins = nc.scalar.activation(prod[:, s % 2, FQ * k + i, :], ring[:, b, i * H:(i + 1) * H],
                                               ACT.Copy, scale=xr[:, s, f:f + 1])
                ins.then_inc(act_done, 1)

            def xt_out(turn, ns):
                for n in ns:
                    if n == D // 4 - 1 and not isinstance(turn, int):
                        src = cur0_ps[0:KX, :]
                    else:
                        src = ring[0:KX, n if isinstance(turn, int) else bank(("X", n), True), :]
                    act.wait_ge(xt_mm, turn * 4 + (n + 1))
                    nc.scalar.activation(
                        xt[0:KX, :].rearrange("p (t d b) -> p d t b", d=D, b=B8)[:, 4 * n:4 * n + 4],
                        src.rearrange("p (d t b) -> p d t b", d=4, b=B8),
                        ACT.Copy).then_inc(xt_done, 1)

            def xs_copy(g, gi, turn):
                if not isinstance(g, int) or g > 0:
                    act.wait_ge(b_mm, g * NJ)
                act.wait_ge(xt_done, turn * 4 + 4)
                src = xt[0:KX, bass.ts(gi, GROWS)]
                nc.scalar.activation(xs[0:KX, :], src, ACT.Copy).then_inc(xs_done, 1)

            def a3_out(g, b):
                act.wait_ge(a3_mm, g + 1)
                nc.scalar.activation(a3[0:NPAIR, :], ring[0:NPAIR, b, :], ACT.Copy).then_inc(a3_done, 1)

            def xr_stage(g, b):
                act.wait_ge(xr_mm, g + 1)
                nc.scalar.activation(xr_next[:, :, 0:NF],
                                     ring[:, b, 0:GT * F1].rearrange("p (t f) -> p t f", f=F1)[:, :, 0:NF],
                                     ACT.Copy).then_inc(xrn_done, 1)

            def xr_out(g, lo, hi):
                if not isinstance(g, int) or g > 0:
                    act.wait_ge(act_done, g * (GT * len(ACT_Q)) - (GT - hi) * len(ACT_Q))
                    act.wait_ge(dve_done, g * (GT * len(DVE_Q)) - (GT - hi) * len(DVE_Q))
                    act.wait_ge(xbd_done, g * GT - (GT - hi))
                act.wait_ge(xrn_done, g + 1)
                nc.scalar.activation(xr[:, lo:hi, 0:NF], xr_next[:, lo:hi, 0:NF], ACT.Copy).then_inc(xr_done, 1)

            def chi_out(g, lo, hi):
                act.wait_ge(z_used, g * NJ + NJ)
                if hi == GT:
                    act.wait_ge(summed0, g + 1)
                if not isinstance(g, int) or g > 0:
                    act.wait_ge(t_ready, g * (GT * NQ) - (GT - hi) * NQ)
                nc.scalar.activation(chi[:, lo * P:hi * P], cur0_ps[:, lo * P:hi * P],
                                     ACT.Copy).then_inc(chi_done, 1)

            def s_out(t, last_turn, b):
                act.wait_ge(s_mm, t + (START + 1))
                nc.scalar.activation(s_sb[:, :, bass.ts(t - (NTURN - 1) * TG * GT if last_turn else t, B8)],
                                     ring[:, b, 0:F1 * B8].rearrange("p (f b) -> p f b", b=B8), ACT.Copy).then_inc(s_done, 1)

            def out2_out():
                act.wait_ge(out2_mm, 1)
                nc.scalar.activation(z1t[:, 0:B - P], s_sb[:, NF, :], ACT.Copy).then_inc(z1_done, 1)
                nc.scalar.activation(z2t[:, 0:B - P], cur0_ps[:, 0:B - P], ACT.Copy).then_inc(out2_done, 1)

            def body(turn, gi, turns, last):
                g = turn * TG + gi
                for n in range(1, GT if last else GT + 1):
                    t, s = g * GT + n, n % GT
                    act.wait_ge(cur1_done, t + (START - 1))
                    for k in range(len(ACT_Q)):
                        multiply(t, s, k, bank(("T", n, ACT_Q[k]), turns, last))
                        if last:
                            continue
                        at = (n - 1) * len(ACT_Q) + k
                        if turns and at in XT_OUT_AFTER:
                            xt_out(turn + 1, (0, 1) if at == XT_OUT_AFTER[0] else (2, 3))
                        if at == XS_AFTER[turns]:
                            if turns:
                                xs_copy(g + 1, 0, turn + 1)
                            else:
                                xs_copy(g + 1, gi + 1, turn)
                        if at == A3_OUT_AFTER[turns]:
                            a3_out(g + 1, bank(("A",), turns))
                        if at == XR_STAGE_AFTER[turns]:
                            xr_stage(g + 1, bank(("R",), turns))
                        if at == XR_OUT_AFTER[0]:
                            xr_out(g + 1, 0, GT - 1)
                        if at == CHI_AFTER[0]:
                            chi_out(g + 1, 0, GT - 1)
                        if at == CHI_AFTER[1]:
                            chi_out(g + 1, GT - 1, GT)
                        if at == XR_OUT_AFTER[1]:
                            xr_out(g + 1, GT - 1, GT)
                    s_out(t - 1, isinstance(turn, int), bank(("S", n), turns, last))

            act.sem_inc(s_done, START)
            act.dma_start(w1_stage.rearrange("p (f m) -> p f m", m=H),
                          w1.rearrange("(f h) m -> h f m", h=H)).then_inc(w1_in, 16)
            act.wait_ge(w1_in, 16)
            nc.scalar.activation(w1hi[:, :], w1_stage, ACT.Copy).then_inc(w1hi_done, 1)
            xt_out(0, range(D // 4))
            xs_copy(0, 0, 0)
            a3_out(0, 4)
            xr_stage(0, 5)
            xr_out(0, 0, GT - 1)
            xr_out(0, GT - 1, GT)
            chi_out(0, 0, GT - 1)
            chi_out(0, GT - 1, GT)
            act.wait_ge(consts_done, 3)
            act.wait_ge(w0_done, 1)
            for k in range(len(ACT_Q)):
                multiply(0, 0, k, TAIL["T", GT, ACT_Q[k]] % NR)
            walk(act, body, out2_out)
            s_out(NG * GT - 1, True, 5)
            act.wait_ge(s_done, NG * GT + START)
            nc.scalar.activation(z1t[:, B - P:B], s_sb[:, NF, 0:P], ACT.Copy).then_inc(z1_done, 1)
            act.wait_ge(out2_mm, 2)
            nc.scalar.activation(z2t[:, B - P:B], cur0_ps[:, 0:P], ACT.Copy).then_inc(out2_done, 1)
            for n in range(HID1 // P):
                act.wait_ge(h1_mm, n + 1)
                nc.scalar.activation(h1t[:, n, :], ring[:, n, :], ACT.Relu, bias=b1_sb[:, n:n + 1]).then_inc(h1_done, 1)
            for n in range(HID2 // P):
                act.wait_ge(h2_mm, n + 1)
                nc.scalar.activation(h2t[:, n, :], ring[:, 4 + n, :], ACT.Relu, bias=b2_sb[:, n:n + 1]).then_inc(h2_done, 1)
            act.wait_ge(y_mm, 1)
            nc.scalar.activation(y_sb, ring[0:1, 6, :], ACT.Copy).then_inc(y_done, 1)

        @block.vector
        def _(dve):
            def split_e(turn):
                dve.wait_ge(gathered, turn * (16 * NF) + 16 * NF)
                if not isinstance(turn, int) or turn > 0:
                    dve.wait_ge(xt_mm, turn * 4)
                src = e_sb[:, :, :].rearrange("p f d -> p d f")
                nc.vector.tensor_copy(e2[:, :, 0:NF].bitcast(F32R), src).then_inc(e2_hi, 1)
                dve.wait_ge(e2_hi, turn + 1)
                nc.vector.tensor_tensor(e2[:, :, LO:KX], src, e2[:, :, 0:NF], ALU.subtract).then_inc(e2_done, 1)

            def pair_product(g, j, b):
                dve.wait_ge(b_mm, g * NJ + (j + 1))
                if j == 0:
                    dve.wait_ge(a3_done, g + 1)
                if not isinstance(g, int) or g > 0 or j >= NZ:
                    dve.wait_ge(z_used, g * NJ + max(j - NZ + 1, 0))
                n = NPAIR if j < NJ - 1 else LASTP
                nc.vector.tensor_tensor(z[0:n, j % NZ, :], ring[0:n, b, :], a3[0:n, :], ALU.mult).then_inc(z_done, 1)

            def clo_out(g, lo, hi):
                dve.wait_ge(chi_done, g * 2 + (1 if hi < GT else 2))
                c = slice(lo * P, hi * P)
                nc.vector.tensor_tensor(clo[:, c], cur0_ps[:, c], chi[:, c].bitcast(F32),
                                        ALU.subtract).then_inc(clo_done, 1)

            def sum_cur0(g):
                dve.wait_ge(z_used, g * NJ + NJ)
                nc.vector.tensor_reduce(z0t[:, bass.ts(g, GT * B8)].rearrange("p (t b) -> p t b", b=B8),
                                        cur0_ps[:, :].rearrange("p (t d b) -> p t b d", d=D, b=B8),
                                        AX.X, ALU.add).then_inc(summed0, 1)

            def fused(t, s, k, b):
                q = DVE_Q[k]
                dve.wait_ge(t_ready, t * NQ + (q + 1))
                dve.wait_ge(act_done, t * len(ACT_Q) + (k + 1))
                for i, f in enumerate(fields(q)):
                    v = prod[:, s % 2, FQ * k + i, :]
                    ins = nc.vector.scalar_tensor_tensor(out=v, in0=ring[:, b, i * H:(i + 1) * H],
                                                         scalar=xr[:, s, f:f + 1], in1=v,
                                                         op0=ALU.mult, op1=ALU.add)
                ins.then_inc(dve_done, 1)

            def halve(t, s):
                dve.wait_ge(act_done, t * len(ACT_Q) + len(ACT_Q))
                dve.wait_ge(dve_done, t * len(DVE_Q) + len(DVE_Q))
                v = prod[:, s % 2, :, :]
                n = NSLOT - HALF
                nc.vector.tensor_tensor(v[:, 0:n, :], v[:, 0:n, :], v[:, HALF:NSLOT, :], ALU.add).then_inc(halved, 1)

            def body(turn, gi, turns, last):
                g = turn * TG + gi
                for n in range(1, GT if last else GT + 1):
                    t, s = g * GT + n, n % GT
                    if n == 1 and turns:
                        split_e(turn + 1)
                    for k in range(len(DVE_Q)):
                        fused(t, s, k, bank(("T", n, DVE_Q[k]), turns, last))
                        at = (n - 1) * len(DVE_Q) + k
                        if last:
                            continue
                        for j, x in enumerate(PRODUCT_AFTER[turns]):
                            if x == at:
                                pair_product(g + 1, j, bank(("B", j), turns))
                        if at == CLO_AFTER[0]:
                            clo_out(g + 1, 0, GT - 1)
                        if at == SUM_AFTER:
                            sum_cur0(g + 1)
                        if at == CLO_AFTER[1]:
                            clo_out(g + 1, GT - 1, GT)
                    halve(t, s)

            dve.wait_ge(const_in, 16)
            nc.vector.tensor_copy(ident[:, :], c_stage[:, C_ID:C_ID + P]).then_inc(consts_done, 1)
            nc.vector.tensor_copy(mask[:, :], c_stage[:, C_MASK:C_MASK + B8]).then_inc(consts_done, 1)
            nc.vector.tensor_copy(sel[:, :], c_stage[:, C_SEL:NC_CONST]).then_inc(consts_done, 1)
            dve.wait_ge(w0_in, 32)
            nc.vector.tensor_tensor(w0s[0:NPAIR, :], w0a_st[0:NPAIR, :], w0b_st[0:NPAIR, :], ALU.add).then_inc(w0_added, 1)
            dve.wait_ge(w0_added, 1)
            nc.vector.tensor_copy(w0s[0:NF, 0:H], w0a_st[0:NF, 0:H]).then_inc(w0_done, 1)
            dve.wait_ge(w1hi_done, 1)
            nc.vector.tensor_tensor(w1lo[:, :], w1_stage, w1hi[:, :].bitcast(F32), ALU.subtract).then_inc(w1lo_done, 1)
            split_e(0)
            for j in range(NJ):
                pair_product(0, j, (6 + j) % NR)
            clo_out(0, 0, GT - 1)
            sum_cur0(0)
            clo_out(0, GT - 1, GT)
            for k in range(len(DVE_Q)):
                fused(0, 0, k, TAIL["T", GT, DVE_Q[k]] % NR)
            halve(0, 0)
            walk(dve, body)

        @block.tensor
        def _(pe):
            def freed(x, g, n0=0, turn=0):
                if x[0] == "T":
                    t, q = g * GT + (x[1] - n0), x[2]
                    if q in ACT_Q:
                        pe.wait_ge(act_done, t * len(ACT_Q) + (ACT_Q.index(q) + 1))
                    else:
                        pe.wait_ge(dve_done, t * len(DVE_Q) + (DVE_Q.index(q) + 1))
                elif x[0] == "S":
                    pe.wait_ge(s_done, g * GT + (x[1] - n0 + START))
                elif x[0] == "X":
                    pe.wait_ge(xt_done, turn * 4 + (4 + x[1] + 1))
                elif x[0] == "A":
                    pe.wait_ge(a3_done, g + 2)
                elif x[0] == "B":
                    pe.wait_ge(z_done, g * NJ + (NJ + x[1] + 1))
                elif x[0] == "R":
                    pe.wait_ge(xrn_done, g + 2)

            def transposes(turn, n, to):
                pe.wait_ge(e2_done, turn + 1)
                for i in range(4):
                    ins = nc.tensor.transpose(to[0:KX, i * P:(i + 1) * P], e2[:, 4 * n + i, :], ident[:, :])
                ins.then_inc(xt_mm, 1)

            def spread_a(g, b):
                pe.wait_ge(xs_done, g + 1)
                nc.tensor.matmul(ring[0:NPAIR, b, :], sel[0:KX, 0:NPAIR], xs[0:KX, :],
                                 start=True, stop=True).then_inc(a3_mm, 1)

            def row_major(g, b):
                for i in range(GT):
                    ins = nc.tensor.matmul(ring[:, b, i * F1:(i + 1) * F1], xs[0:KX, i * P:(i + 1) * P], selx,
                                           start=True, stop=True, skip_group_check=True)
                ins.then_inc(xr_mm, 1)

            def spread_b(g, j, b):
                c = (1 + j) * NPAIR
                nc.tensor.matmul(ring[0:NPAIR, b, :], sel[0:KX, c:c + NPAIR], xs[0:KX, :],
                                 start=True, stop=True).then_inc(b_mm, 1)

            def contract0(g, j):
                if j == 0 and (not isinstance(g, int) or g > 0):
                    pe.wait_ge(clo_done, g * 2)
                pe.wait_ge(z_done, g * NJ + (j + 1))
                n = NPAIR if j < NJ - 1 else LASTP
                nc.tensor.matmul(cur0_ps[:, :], w0s[0:n, j * H:(j + 1) * H], z[0:n, j % NZ, :],
                                 start=(j == 0), stop=(j == NJ - 1)).then_inc(z_used, 1)

            def contract1(s, q, b):
                c = slice(s * P, (s + 1) * P)
                w = slice(FQ * q * H, (fields(q)[-1] + 1) * H)
                o = ring[:, b, 0:w.stop - w.start]
                nc.tensor.matmul(o, chi[:, c], w1hi[:, w], start=True, stop=False)
                nc.tensor.matmul(o, chi[:, c], w1lo[:, w], start=False, stop=False)
                nc.tensor.matmul(o, clo[:, c], w1hi[:, w], start=False, stop=True).then_inc(t_ready, 1)

            def contract_d(t, s, b):
                u = s % 2
                pe.wait_ge(cur1_done, t + (START + 1))
                pe.wait_ge(xbd_done, t + 1)
                nc.tensor.matmul(ring[:, b, 0:F1 * B8], cur1[:, u, :], xbd[:, u, :, :].rearrange("p f b -> p (f b)"),
                                 start=True, stop=True).then_inc(s_mm, 1)

            def layer2(n):
                for f in range(NF):
                    ins = nc.tensor.matmul(cur0_ps[:, 0:n], w2_sb[:, f, :], s_sb[:, f, 0:n],
                                           start=(f == 0), stop=(f == NF - 1))
                ins.then_inc(out2_mm, 1)

            def layer2_turns():
                pe.wait_ge(clo_done, 2 * (NG - TG + 1))
                pe.wait_ge(s_done, (NG - TG) * GT + START)
                layer2(B - P)

            def hidden1(k, w, x, last=False):
                for n in range(HID1 // P):
                    ins = nc.tensor.matmul(ring[:, n, :], w[:, n * P:(n + 1) * P], x, start=(k == 0), stop=last)
                    if last:
                        ins.then_inc(h1_mm, 1)

            def body(turn, gi, turns, last):
                g = turn * TG + gi
                steps, place = PLANS[2 if last else int(turns)]
                holder = {v % NR: (k, 0) for k, v in TAIL.items() if v >= -NR}
                for x in steps:
                    b = place[x] % NR if x in place else None
                    if x in place:
                        y, ended = holder[b]
                        freed(y, g, 0 if ended else GT, turn)
                        holder[b] = (x, 1)
                    if x[0] == "T":
                        n, q = x[1:]
                        if n == 3 and q == 0:
                            pe.wait_ge(clo_done, g * 2 + 2)
                        if n == 4 and q == 0:
                            pe.wait_ge(clo_done, g * 2 + 3)
                        contract1(n % GT, q, b)
                    elif x[0] == "S":
                        contract_d(g * GT + (x[1] - 1), x[1] - 1, b)
                    elif x[0] == "X":
                        if b is None:
                            pe.wait_ge(clo_done, g * 2 + 2)
                        transposes(turn + 1, x[1], cur0_ps if b is None else ring[:, b, :])
                    elif x[0] == "A":
                        spread_a(g + 1, b)
                    elif x[0] == "B":
                        spread_b(g + 1, x[1], b)
                    elif x[0] == "R":
                        row_major(g + 1, b)
                    else:
                        contract0(g + 1, x[1])

            pe.sem_inc(s_mm, START)
            pe.wait_ge(consts_done, 3)
            pe.wait_ge(padded, 2)
            for n in range(D // 4):
                transposes(0, n, ring[:, n, :])
            spread_a(0, 4)
            row_major(0, 5)
            for j in range(5):
                spread_b(0, j, (6 + j) % NR)
            pe.wait_ge(w0_done, 1)
            for j in range(NJ):
                contract0(0, j)
                if j == 0:
                    pe.wait_ge(a3_done, 1)
                    spread_b(0, 5, 4)
                if j == 1:
                    pe.wait_ge(xrn_done, 1)
                    spread_b(0, 6, 5)
            pe.wait_ge(clo_done, 1)
            pe.wait_ge(w1lo_done, 1)
            for q in range(NQ):
                y = next((r for r in range(q) if (TAIL["T", GT, q] - TAIL["T", GT, r]) == NR), None)
                if y is not None:
                    freed(("T", 0, y), 0)
                contract1(0, q, TAIL["T", GT, q] % NR)
            pe.wait_ge(w2_in, 16)
            walk(pe, body, layer2_turns)
            pe.wait_ge(top_in, 7 * 16)
            pe.wait_ge(summed0, NG)
            pe.wait_ge(act_done, NG * GT * len(ACT_Q))
            pe.wait_ge(dve_done, NG * GT * len(DVE_Q))
            pe.wait_ge(s_done, NG * GT - 1 + START)
            hidden1(0, wt1d_sb, dt_sb)
            hidden1(1, wt1_sb[:, 0, :], z0t[:, :])
            contract_d(NG * GT - 1, GT - 1, 5)
            pe.wait_ge(s_done, NG * GT + START)
            layer2(P)
            pe.wait_ge(z1_done, 2)
            hidden1(2, wt1_sb[:, 1, :], z1t)
            pe.wait_ge(out2_done, 2)
            hidden1(3, wt1_sb[:, 2, :], z2t, last=True)
            for n in range(HID2 // P):
                for k in range(HID1 // P):
                    if n == 0:
                        pe.wait_ge(h1_done, k + 1)
                    ins = nc.tensor.matmul(ring[:, 4 + n, :], wt2_sb[:, k, n * P:(n + 1) * P], h1t[:, k, :],
                                           start=(k == 0), stop=(k == HID1 // P - 1))
                ins.then_inc(h2_mm, 1)
            for k in range(HID2 // P):
                pe.wait_ge(h2_done, k + 1)
                ins = nc.tensor.matmul(ring[0:1, 6, :], wt3_sb[:, k:k + 1], h2t[:, k, :],
                                       start=(k == 0), stop=(k == HID2 // P - 1))
            ins.then_inc(y_mm, 1)


def _constants():
    import numpy as np
    c = np.zeros((P, NC_CONST), np.float32)
    c[:, C_ID:C_ID + P] = np.eye(P)
    for row in range(P):
        c[row, C_MASK + row % B8] = 1.0
    for p in range(NPAIR):
        f = p % NF
        for r in (f, LO + f):
            c[r, C_SEL + p] = 1.0
        for j in range(NJ):
            g = (f + KREP * j + p // NF) % NF
            for r in (g, LO + g):
                c[r, C_SEL + (1 + j) * NPAIR + p] = 1.0
    for f in range(NF):
        for r in (f, LO + f):
            c[r, C_SELX + f] = 1.0
    return c


def kernel(**inputs):
    import numpy as np
    import concourse.bacc as bacc
    from concourse.bass_utils import run_bass_kernel_spmd

    f0 = np.asarray(inputs["L0_rec_f0"])
    w0a = np.zeros((NPAIR, NJ, H), f0.dtype)
    w0b = np.zeros((NPAIR, NJ, H), f0.dtype)
    for j in range(NJ):
        for kk in range(KREP):
            k = KREP * j + kk
            if k < NK:
                f = np.arange(NF)
                g = (f + k) % NF
                w0a[kk * NF:(kk + 1) * NF, j] = f0[f * NF + g]
                w0b[kk * NF:(kk + 1) * NF, j] = f0[g * NF + f]

    nc = bacc.Bacc("TRN2", target_bir_lowering=False, num_devices=1)
    arrays = {}

    def dram(name, a):
        a = np.ascontiguousarray(a)
        arrays[name] = a
        return nc.dram_tensor(name, a.shape, mybir.dt.from_np(a.dtype), kind="ExternalInput").ap()

    def by_partition(a):
        return np.asarray(a).reshape(-1, P).T

    args = [
        dram("ids", inputs["ids"]),
        [dram(f"tbl_{f}", inputs[f"tbl_{f}"]) for f in range(NF)],
        dram("consts", _constants()),
        dram("w0a", w0a), dram("w0b", w0b),
        dram("w1", inputs["L0_rec_f1"]), dram("w2", inputs["L0_rec_f2"]),
        dram("dense_t", np.asarray(inputs["dense_ctx"]).T),
        dram("w_top1", inputs["W_top1"]), dram("b_top1", by_partition(inputs["b_top1"])),
        dram("w_top2", inputs["W_top2"]), dram("b_top2", by_partition(inputs["b_top2"])),
        dram("w_top3", by_partition(inputs["W_top3"])),
        nc.dram_tensor("y", (1, B), F32, kind="ExternalOutput").ap(),
    ]
    build(nc, *args)
    return run_bass_kernel_spmd(nc, [arrays], core_ids=[0]).results[0]["y"].reshape(B, 1)
```

```python
from contextlib import ExitStack

import concourse.bass as bass
from concourse import mybir

ALU = mybir.AluOpType
ACT = mybir.ActivationFunctionType
AX = mybir.AxisListType
F32 = mybir.dt.float32
F32R = mybir.dt.float32r
I32 = mybir.dt.int32
U32 = mybir.dt.uint32

P = 128
NF = 39
D = 16
B = 512
H = 128
B8 = P // D
GT = 4
NG = B // (B8 * GT)
TG = P // (B8 * GT)
NTURN = NG // TG
GROWS = GT * P
LO = 64
KX = LO + NF
NPAIR = P
NPAIRS = NF * (NF + 1) // 2
NJ = NPAIRS // P + 1
NREST = NPAIRS - (NJ - 1) * P
COPIES = (0, 32, 64)
LASTP = COPIES[-1] + NREST
FQ = 4
NQ = (NF + FQ - 1) // FQ
ACT_Q = [0, 2, 4, 5, 7, 9]
DVE_Q = [1, 3, 6, 8]
NZ = 4

TRANSPOSE_AT = ([], [29, 30, 33, 38])
SPREAD_A_AT = (3, 3)
ROW_MAJOR_AT = (12, 17)
SPREAD_AT = ([3, 4, 7, 9, 14, 17, 19], [3, 4, 7, 8, 13, 13, 18])
CONTRACT_AT = ([8, 10, 12, 17, 20, 27, 27], [9, 10, 16, 17, 23, 25, 27])
PRODUCT_AFTER = ([0, 0, 2, 3, 4, 6, 7], [0, 0, 2, 3, 5, 5, 7])
ZHI_AFTER = ([1, 2, 4, 6, 9, 11, 13], [2, 3, 4, 6, 8, 9, 13])
ZLO_AFTER = ([1, 2, 3, 4, 6, 8, 8], [2, 2, 3, 5, 6, 7, 8])
SPLIT_AFTER = 8
XT_OUT_AFTER = (18, 22)
XS_AFTER = (0, 0)
A3_OUT_AFTER = (0, 0)
XR_STAGE_AFTER = (6, 9)
XR_OUT_AFTER = (14, 19)
PIECES = [(0, 1), (1, 3), (3, 4)]
CHI_AFTER = (15, 17, 21)
CLO_AFTER = (10, 12, 14)
SUM_AFTER = 12
S_AFTER = 9

SKIP_AT = ([("T", 1, 1), ("T", 3, 3), ("T", 1, 7)], [])
FRONT = 13
GATHER_TILES = 9
NSLOT = sum(min(FQ, NF - FQ * q) for q in ACT_Q)
HALF = (NSLOT + 1) // 2
EARLY = 33
WARM_PRODUCTS = 17, 8, 7
NR = 7
F1 = NF + 1
HID1, HID2 = 512, 256
ND = 16
C_ID, C_MASK, C_SEL = 0, P, P + B8
C_SELX = C_SEL + (NJ + 1) * NPAIR
NC_CONST = C_SELX + F1


def fields(q):
    return range(FQ * q, min(FQ * q + FQ, NF))


def plan(turns, last=False):
    steps = []
    for n in range(1, GT if last else GT + 1):
        for q in range(NQ):
            steps.append(("T", n, q))
            if q == S_AFTER:
                steps.append(("S", n))
            at = (n - 1) * NQ + q
            if last:
                continue
            steps += [("X", i) for i, x in enumerate(TRANSPOSE_AT[turns]) if x == at]
            steps += [("A",)] * (SPREAD_A_AT[turns] == at)
            steps += [("C", j) for j, x in enumerate(CONTRACT_AT[turns]) if x == at]
            steps += [("B", j) for j, x in enumerate(SPREAD_AT[turns]) if x == at]
            steps += [("R",)] * (ROW_MAJOR_AT[turns] == at)
    ring = [x for x in steps if x[0] != "C" and x != ("X", 3)]
    place, at = {}, 0
    for x in ring:
        at += (x in SKIP_AT[turns] and not last)
        place[x] = at
        at += 1
    assert last or at % NR == 0, at
    return steps, place


PLANS = [plan(0), plan(1), plan(0, True)]
assert all(PLANS[0][1][x] % NR == b % NR for x, b in PLANS[1][1].items() if b >= max(PLANS[1][1].values()) - NR + 1)
TAIL = {k: v - (max(PLANS[0][1].values()) + 1) for k, v in PLANS[0][1].items()}
TAIL = {k: v for k, v in TAIL.items() if k[0] in "TS" and k[1] == GT}


def build(nc, ids, tables, consts, w0a, w0b, w1, w2, dense_t, wt1, bt1, wt2, bt2, wt3, out):
    with ExitStack() as ctx:
        def sb(name, shape, dt=F32):
            return ctx.enter_context(nc.sbuf_tensor(name, shape, dt))

        def ps(name, shape):
            return ctx.enter_context(nc.psum_tensor(name, shape, F32))

        def sem(name):
            return ctx.enter_context(nc.semaphore(name))

        ring = ps("ring", [P, NR, 512])
        cur0_ps = ps("cur0_ps", [P, 512])

        w1hi = sb("w1hi", [P, NF * H], F32R)
        w2_sb = sb("w2_sb", [P, NF, H])
        s_sb = sb("s_sb", [P, F1, B - P])
        w1_stage = s_sb[:, :, :].rearrange("p f b -> p (f b)")[:, 0:NF * H]
        prod = sb("prod", [P, 2, NSLOT, H])
        stage = prod[:, :, :, :].rearrange("p a s m -> p (a s m)")
        c_stage = stage[:, 0:NC_CONST]
        w0a_st = stage[:, NC_CONST:NC_CONST + NJ * H]
        w0b_st = stage[:, NC_CONST + NJ * H:NC_CONST + 2 * NJ * H]
        ident = sb("ident", [P, P], F32R)
        mask = sb("mask", [P, B8])
        sel = sb("sel", [P, NC_CONST - C_SEL], F32R)
        selx = sel[0:KX, C_SELX - C_SEL:C_SELX - C_SEL + F1]
        w0hi = sb("w0hi", [P, NJ * H], F32R)
        w0lo = sb("w0lo", [P, NJ * H], F32R)
        idx = sb("idx", [P, NF], I32)
        e_sb = sb("e_sb", [P, NF, D])
        e2 = sb("e2", [P, D, KX], F32R)
        xt = sb("xt", [P, TG * GROWS], F32R)
        xs = sb("xs", [P, GROWS], F32R)
        a3 = sb("a3", [P, GROWS])
        z = sb("z", [P, 2, GROWS])
        zhi = sb("zhi", [P, NZ, GROWS], F32R)
        zlo = sb("zlo", [P, NZ, GROWS], F32R)
        chi = sb("chi", [P, GROWS], F32R)
        clo = sb("clo", [P, GROWS], F32R)
        xr = sb("xr", [P, GT, F1])
        xr_next = sb("xr_next", [P, GT, F1])
        xbd = sb("xbd", [P, 2, F1, B8])
        cur1 = sb("cur1", [P, 2, H])
        z0t = sb("z0t", [P, B])
        z1t = e_sb[:, :, :].rearrange("p f d -> p (f d)")[:, 0:B]
        z2t = sb("z2t", [P, B])[:, :]
        wt3_sb = sb("wt3_sb", [P, HID2 // P])
        b1_sb = sb("b1_sb", [P, HID1 // P])
        b2_sb = sb("b2_sb", [P, HID2 // P])
        h1t = stage[:, 0:HID1 // P * B].rearrange("p (n b) -> p n b", b=B)
        h2t = stage[:, HID1 // P * B:(HID1 + HID2) // P * B].rearrange("p (n b) -> p n b", b=B)
        y_sb = a3[0:1, :]
        w1lo = sb("w1lo", [P, NF * H], F32R)
        wt1_sb = xt[:, 0:3 * HID1].bitcast(F32).rearrange("p (k n) -> p k n", n=HID1)
        dt_sb = xt[0:ND, 3 * HID1:3 * HID1 + B].bitcast(F32)
        wt2_sb = z[:, :, :].rearrange("p a (k n) -> p (a k) n", n=HID2)
        wt1d_sb = a3[0:ND, :]

        START = 1
        idx_in = sem("idx_in")
        const_in = sem("const_in")
        w0_in = sem("w0_in")
        w1_in = sem("w1_in")
        w2_in = sem("w2_in")
        top_in = sem("top_in")
        gathered_early = sem("gathered_early")
        gathered_late = sem("gathered_late")
        gathered = sem("gathered")
        padded = sem("padded")
        e2_padded = sem("e2_padded")
        consts_done = sem("consts_done")
        w0_added = sem("w0_added")
        w0_folded = sem("w0_folded")
        w0_done = sem("w0_done")
        w1hi_done = sem("w1hi_done")
        w1lo_done = sem("w1lo_done")
        e2_hi = sem("e2_hi")
        e2_done = sem("e2_done")
        xt_mm = sem("xt_mm")
        xt_done = sem("xt_done")
        xs_done = sem("xs_done")
        a3_mm = sem("a3_mm")
        a3_done = sem("a3_done")
        xr_mm = sem("xr_mm")
        xrn_done = sem("xrn_done")
        xr_done = sem("xr_done")
        b_mm = sem("b_mm")
        z_done = sem("z_done")
        zhi_done = sem("zhi_done")
        zlo_done = sem("zlo_done")
        z_used = sem("z_used")
        chi_done = sem("chi_done")
        clo_done = sem("clo_done")
        summed0 = sem("summed0")
        t_ready = sem("t_ready")
        act_done = sem("act_done")
        dve_done = sem("dve_done")
        halved = sem("halved")
        pool_step = sem("pool_step")
        cur1_done = sem("cur1_done")
        xbd_done = sem("xbd_done")
        s_mm = sem("s_mm")
        s_done = sem("s_done")
        out2_mm = sem("out2_mm")
        z1_done = sem("z1_done")
        out2_done = sem("out2_done")
        h1_mm = sem("h1_mm")
        h1_done = sem("h1_done")
        h2_mm = sem("h2_mm")
        h2_done = sem("h2_done")
        y_mm = sem("y_mm")
        y_done = sem("y_done")
        y_out = sem("y_out")

        block = ctx.enter_context(nc.Block())

        def bank(x, turns, last=False):
            return PLANS[2 if last else int(turns)][1][x] % NR

        def top_bank(i):
            return (max(PLANS[2][1].values()) + 1 + i) % NR

        h1_ps = [ring[:, top_bank(n), :] for n in range(HID1 // P)]
        y_ps = ring[0:1, top_bank(4), :]
        h2_ps = [ring[:, top_bank(5 + n), :] for n in range(HID2 // P)]

        def walk(eng, body, before_last=None):
            with eng.Fori(0, NTURN - 1) as turn:
                with eng.Fori(0, TG - 2) as gi:
                    body(turn, gi, False, False)
                body(turn, TG - 2, True, False)
                body(turn, TG - 1, False, False)
            if before_last:
                before_last()
            with eng.Fori(0, TG - 1) as gi:
                body(NTURN - 1, gi, False, False)
            body(NTURN - 1, TG - 1, False, True)

        @block.sync
        def _(sp):
            sp.dma_start(idx[:, :], ids[0:P, :]).then_inc(idx_in, 16)
            sp.dma_start(c_stage, consts).then_inc(const_in, 16)
            sp.dma_start(w0a_st[0:NPAIR, :].rearrange("p (j m) -> p j m", m=H), w0a).then_inc(w0_in, 16)
            sp.dma_start(w0b_st[0:NPAIR, :].rearrange("p (j m) -> p j m", m=H), w0b).then_inc(w0_in, 16)
            sp.dma_start(w2_sb[:, :, :], w2.rearrange("(f h) m -> h f m", h=H)).then_inc(w2_in, 16)
            sp.dma_start(wt3_sb[:, :], wt3).then_inc(top_in, 16)
            sp.dma_start(b1_sb[:, :], bt1).then_inc(top_in, 16)
            sp.dma_start(b2_sb[:, :], bt2).then_inc(top_in, 16)
            sp.wait_ge(gathered_early, 16 * EARLY)
            sp.wait_ge(gathered_late, 16 * (NF - EARLY))
            sp.dma_start(idx[:, :], ids[P:2 * P, :]).then_inc(idx_in, 16)
            with sp.Fori(2, NTURN) as turn:
                sp.wait_ge(gathered, turn * (16 * NF) - 16 * NF)
                sp.dma_start(idx[:, :], ids[bass.ts(turn, P), :]).then_inc(idx_in, 16)
            sp.wait_ge(zlo_done, NG * NJ)
            sp.wait_ge(xs_done, NG)
            sp.dma_start(wt1_sb[:, :, :], wt1[0:3 * P, :].rearrange("(k p) n -> p k n", p=P)).then_inc(top_in, 16)
            sp.dma_start(wt1d_sb, wt1[3 * P:3 * P + ND, :]).then_inc(top_in, 16)
            sp.dma_start(dt_sb, dense_t).then_inc(top_in, 16)
            sp.dma_start(wt2_sb[:, :, :], wt2.rearrange("(k p) n -> p k n", p=P)).then_inc(top_in, 16)
            sp.wait_ge(y_done, 1)
            sp.dma_start(out, y_sb).then_inc(y_out, 16)
            sp.wait_ge(y_out, 16)

        @block.gpsimd
        def _(pool):
            def gather(fs, done=gathered):
                for f in fs:
                    nc.gpsimd.indirect_dma_start(
                        out=e_sb[:, f, :], out_offset=None, in_=tables[f],
                        in_offset=bass.IndirectOffsetOnAxis(ap=idx[:, f:f + 1].bitcast(U32), axis=0),
                    ).then_inc(done, 16)

            def tile(t, s, xr_count):
                u = s % 2
                v = prod[:, u, :, :]
                pool.wait_ge(xr_done, xr_count)
                if not isinstance(t, int) or t >= 2:
                    pool.wait_ge(s_mm, t + (START - 1))
                nc.gpsimd.tensor_tensor(
                    xbd[:, u, :, :],
                    xr[:, s, :].rearrange("p (f o) -> p f o", o=1).broadcast_to([P, F1, B8]),
                    mask[:, :].rearrange("p (o b) -> p o b", o=1).broadcast_to([P, F1, B8]),
                    ALU.mult).then_inc(xbd_done, 1)
                n = HALF // 3
                pool.wait_ge(halved, t * 2 + 1)
                nc.gpsimd.tensor_tensor(v[:, 0:n, :], v[:, 0:n, :], v[:, n:2 * n, :], ALU.add).then_inc(pool_step, 1)
                pool.wait_ge(pool_step, t * 3 + 1)
                pool.wait_ge(halved, t * 2 + 2)
                nc.gpsimd.tensor_tensor(v[:, 0:n, :], v[:, 0:n, :], v[:, 2 * n:3 * n, :], ALU.add).then_inc(pool_step, 1)
                pool.wait_ge(pool_step, t * 3 + 2)
                nc.gpsimd.tensor_tensor(v[:, 0:2, :], v[:, 0:2, :], v[:, 2:4, :], ALU.add).then_inc(pool_step, 1)
                pool.wait_ge(pool_step, t * 3 + 3)
                nc.gpsimd.tensor_tensor(cur1[:, u, :], v[:, 0, :], v[:, 1, :], ALU.add).then_inc(cur1_done, 1)

            def body(g, gathers=(), last=False):
                for n in range(1, GT if last else GT + 1):
                    tile(g * GT + n, n % GT, g * 2 + (1, 1, 2, 3)[n - 1])
                    if gathers:
                        gather(gathers[n - 1])

            def rest(gi):
                n = NF - FRONT
                return [range(FRONT + min(n * i // GATHER_TILES, n), FRONT + min(n * (i + 1) // GATHER_TILES, n))
                        for i in range(GT * gi, GT * gi + GT)]

            front = [range(FRONT * i // GT, FRONT * (i + 1) // GT) for i in range(GT)]

            pool.sem_inc(cur1_done, START)
            nc.gpsimd.memset(a3[:, 0:D * (LO - NF)], 0.0).then_inc(padded, 1)
            nc.gpsimd.memset(xr[:, :, NF:F1], 1.0).then_inc(padded, 1)
            pool.wait_ge(idx_in, 16)
            gather(range(EARLY), gathered_early)
            gather(range(EARLY, NF), gathered_late)
            pool.wait_ge(consts_done, 3)
            pool.wait_ge(padded, 2)
            pool.wait_ge(idx_in, 32)
            pool.wait_ge(e2_done, 1)
            gather(range(FRONT))
            tile(0, 0, 1)
            with pool.Fori(0, NTURN - 2) as turn:
                for gi in range(TG - 1):
                    body(turn * TG + gi, rest(gi))
                pool.wait_ge(e2_done, turn + 2)
                pool.wait_ge(idx_in, turn * 16 + 48)
                body(turn * TG + TG - 1, front)
            for gi in range(TG - 1):
                body((NTURN - 2) * TG + gi, rest(gi))
            body((NTURN - 2) * TG + TG - 1)
            with pool.Fori(NG - TG, NG - 1) as g:
                body(g)
            body(NG - 1, last=True)

        @block.scalar
        def _(act):
            def multiply(t, s, k, b):
                q = ACT_Q[k]
                act.wait_ge(t_ready, t * NQ + (q + 1))
                for i, f in enumerate(fields(q)):
                    ins = nc.scalar.activation(prod[:, s % 2, FQ * k + i, :], ring[:, b, i * H:(i + 1) * H],
                                               ACT.Copy, scale=xr[:, s, f:f + 1])
                ins.then_inc(act_done, 1)

            def xt_out(turn, ns):
                for n in ns:
                    if n == D // 4 - 1 and not isinstance(turn, int):
                        src = cur0_ps[0:KX, :]
                    else:
                        src = ring[0:KX, n if isinstance(turn, int) else bank(("X", n), True), :]
                    act.wait_ge(xt_mm, turn * 4 + (n + 1))
                    nc.scalar.activation(
                        xt[0:KX, :].rearrange("p (t d b) -> p d t b", d=D, b=B8)[:, 4 * n:4 * n + 4],
                        src.rearrange("p (d t b) -> p d t b", d=4, b=B8),
                        ACT.Copy).then_inc(xt_done, 1)

            def xs_copy(g, gi, turn):
                if not isinstance(g, int) or g > 0:
                    act.wait_ge(b_mm, g * NJ)
                act.wait_ge(xt_done, turn * 4 + 4)
                src = xt[0:KX, bass.ts(gi, GROWS)]
                nc.scalar.activation(xs[0:KX, :], src, ACT.Copy).then_inc(xs_done, 1)

            def a3_out(g, b):
                act.wait_ge(a3_mm, g + 1)
                nc.scalar.activation(a3[0:NPAIR, :], ring[0:NPAIR, b, :], ACT.Copy).then_inc(a3_done, 1)

            def zhi_out(g, j):
                act.wait_ge(z_done, g * NJ + (j + 1))
                act.wait_ge(z_used, g * NJ + max(j - NZ + 1, 0))
                n = NPAIR if j < NJ - 1 else LASTP
                nc.scalar.activation(zhi[0:n, j % NZ, :], z[0:n, j % 2, :], ACT.Copy).then_inc(zhi_done, 1)

            def xr_stage(g, b):
                act.wait_ge(xr_mm, g + 1)
                nc.scalar.activation(xr_next[:, :, 0:NF],
                                     ring[:, b, 0:GT * F1].rearrange("p (t f) -> p t f", f=F1)[:, :, 0:NF],
                                     ACT.Copy).then_inc(xrn_done, 1)

            def xr_out(g, lo, hi):
                if not isinstance(g, int) or g > 0:
                    act.wait_ge(act_done, g * (GT * len(ACT_Q)) - (GT - hi) * len(ACT_Q))
                    act.wait_ge(dve_done, g * (GT * len(DVE_Q)) - (GT - hi) * len(DVE_Q))
                    act.wait_ge(xbd_done, g * GT - (GT - hi))
                act.wait_ge(xrn_done, g + 1)
                nc.scalar.activation(xr[:, lo:hi, 0:NF], xr_next[:, lo:hi, 0:NF], ACT.Copy).then_inc(xr_done, 1)

            def chi_out(g, i):
                lo, hi = PIECES[i]
                act.wait_ge(z_used, g * NJ + NJ)
                if i > 0:
                    act.wait_ge(clo_done, g * len(PIECES) + i)
                if hi == GT:
                    act.wait_ge(summed0, g + 1)
                if not isinstance(g, int) or g > 0:
                    act.wait_ge(t_ready, g * (GT * NQ) - (GT - hi) * NQ)
                nc.scalar.activation(chi[:, lo * P:hi * P], cur0_ps[:, lo * P:hi * P],
                                     ACT.Copy).then_inc(chi_done, 1)

            def s_out(t, last_turn, b):
                act.wait_ge(s_mm, t + (START + 1))
                nc.scalar.activation(s_sb[:, :, bass.ts(t - (NTURN - 1) * TG * GT if last_turn else t, B8)],
                                     ring[:, b, 0:F1 * B8].rearrange("p (f b) -> p f b", b=B8), ACT.Copy).then_inc(s_done, 1)

            def out2_out():
                act.wait_ge(out2_mm, 1)
                nc.scalar.activation(z1t[:, 0:B - P], s_sb[:, NF, :], ACT.Copy).then_inc(z1_done, 1)
                nc.scalar.activation(z2t[:, 0:B - P], cur0_ps[:, 0:B - P], ACT.Copy).then_inc(out2_done, 1)

            def body(turn, gi, turns, last):
                g = turn * TG + gi
                for n in range(1, GT if last else GT + 1):
                    t, s = g * GT + n, n % GT
                    act.wait_ge(cur1_done, t + (START - 1))
                    for k in range(len(ACT_Q)):
                        multiply(t, s, k, bank(("T", n, ACT_Q[k]), turns, last))
                        if last:
                            continue
                        at = (n - 1) * len(ACT_Q) + k
                        if turns and at in XT_OUT_AFTER:
                            xt_out(turn + 1, (0, 1) if at == XT_OUT_AFTER[0] else (2, 3))
                        if at == XS_AFTER[turns]:
                            if isinstance(gi, int) and gi == TG - 1:
                                xs_copy(g + 1, 0, turn + 1)
                            else:
                                xs_copy(g + 1, gi + 1, turn)
                        if at == A3_OUT_AFTER[turns]:
                            a3_out(g + 1, bank(("A",), turns))
                        for j, x in enumerate(ZHI_AFTER[turns]):
                            if x == at:
                                zhi_out(g + 1, j)
                        if at == XR_STAGE_AFTER[turns]:
                            xr_stage(g + 1, bank(("R",), turns))
                        if at == XR_OUT_AFTER[0]:
                            xr_out(g + 1, 0, GT - 1)
                        for i in range(len(PIECES)):
                            if at == CHI_AFTER[i]:
                                chi_out(g + 1, i)
                        if at == XR_OUT_AFTER[1]:
                            xr_out(g + 1, GT - 1, GT)
                    s_out(t - 1, isinstance(turn, int), bank(("S", n), turns, last))

            act.sem_inc(s_done, START)
            act.sem_inc(zhi_done, NJ)
            act.dma_start(w1_stage.rearrange("p (f m) -> p f m", m=H),
                          w1.rearrange("(f h) m -> h f m", h=H)).then_inc(w1_in, 16)
            act.wait_ge(w1_in, 16)
            nc.scalar.activation(w1hi[:, :], w1_stage, ACT.Copy).then_inc(w1hi_done, 1)
            xt_out(0, range(D // 4))
            xs_copy(0, 0, 0)
            a3_out(0, 4)
            xr_stage(0, 5)
            xr_out(0, 0, GT - 1)
            xr_out(0, GT - 1, GT)
            for i in range(len(PIECES)):
                chi_out(0, i)
            act.wait_ge(consts_done, 3)
            act.wait_ge(w0_done, 1)
            for k in range(len(ACT_Q)):
                multiply(0, 0, k, TAIL["T", GT, ACT_Q[k]] % NR)
            walk(act, body, out2_out)
            s_out(NG * GT - 1, True, top_bank(4))
            act.wait_ge(s_done, NG * GT + START)
            nc.scalar.activation(z1t[:, B - P:B], s_sb[:, NF, 0:P], ACT.Copy).then_inc(z1_done, 1)
            act.wait_ge(out2_mm, 2)
            nc.scalar.activation(z2t[:, B - P:B], cur0_ps[:, 0:P], ACT.Copy).then_inc(out2_done, 1)
            for n in range(HID1 // P):
                act.wait_ge(h1_mm, n + 1)
                nc.scalar.activation(h1t[:, n, :], h1_ps[n], ACT.Relu, bias=b1_sb[:, n:n + 1]).then_inc(h1_done, 1)
            for n in range(HID2 // P):
                act.wait_ge(h2_mm, n + 1)
                nc.scalar.activation(h2t[:, n, :], h2_ps[n], ACT.Relu, bias=b2_sb[:, n:n + 1]).then_inc(h2_done, 1)
            act.wait_ge(y_mm, 1)
            nc.scalar.activation(y_sb, y_ps, ACT.Copy).then_inc(y_done, 1)

        @block.vector
        def _(dve):
            def split_fields(lo, hi, count):
                src = e_sb[:, lo:hi, :].rearrange("p f d -> p d f")
                nc.vector.tensor_copy(e2[:, :, lo:hi], src).then_inc(e2_hi, 1)
                dve.wait_ge(e2_hi, count)
                return nc.vector.tensor_tensor(e2[:, :, LO + lo:LO + hi], src, e2[:, :, lo:hi].bitcast(F32), ALU.subtract)

            def split_e(turn):
                dve.wait_ge(gathered, turn * (16 * NF))
                dve.wait_ge(xt_mm, turn * 4)
                split_fields(0, NF, turn + 2).then_inc(e2_done, 1)

            def pair_product(g, j, b):
                dve.wait_ge(b_mm, g * NJ + (j + 1))
                if j == 0:
                    dve.wait_ge(a3_done, g + 1)
                if not isinstance(g, int):
                    dve.wait_ge(zlo_done, g * NJ + max(j - 1, 0))
                elif j >= 2:
                    dve.wait_ge(z_used, j - 1)
                n = NPAIR if j < NJ - 1 else LASTP
                nc.vector.tensor_tensor(z[0:n, j % 2, :], ring[0:n, b, :], a3[0:n, :], ALU.mult).then_inc(z_done, 1)

            def zlo_out(g, j):
                dve.wait_ge(zhi_done, g * NJ + (j + 1))
                to, rows = (zlo, slice(0, P)) if j < NJ - 1 else (zhi, slice(COPIES[2], LASTP))
                nc.vector.tensor_tensor(to[rows, j % NZ, :], z[rows, j % 2, :], zhi[rows, j % NZ, :].bitcast(F32),
                                        ALU.subtract).then_inc(zlo_done, 1)

            def clo_out(g, i):
                lo, hi = PIECES[i]
                dve.wait_ge(chi_done, g * len(PIECES) + (i + 1))
                c = slice(lo * P, hi * P)
                nc.vector.tensor_tensor(clo[:, c], cur0_ps[:, c], chi[:, c].bitcast(F32),
                                        ALU.subtract).then_inc(clo_done, 1)

            def sum_cur0(g):
                dve.wait_ge(z_used, g * NJ + NJ)
                nc.vector.tensor_reduce(z0t[:, bass.ts(g, GT * B8)].rearrange("p (t b) -> p t b", b=B8),
                                        cur0_ps[:, :].rearrange("p (t d b) -> p t b d", d=D, b=B8),
                                        AX.X, ALU.add).then_inc(summed0, 1)

            def fused(t, s, k, b):
                q = DVE_Q[k]
                dve.wait_ge(t_ready, t * NQ + (q + 1))
                dve.wait_ge(act_done, t * len(ACT_Q) + (k + 1))
                for i, f in enumerate(fields(q)):
                    v = prod[:, s % 2, FQ * k + i, :]
                    ins = nc.vector.scalar_tensor_tensor(out=v, in0=ring[:, b, i * H:(i + 1) * H],
                                                         scalar=xr[:, s, f:f + 1], in1=v,
                                                         op0=ALU.mult, op1=ALU.add)
                ins.then_inc(dve_done, 1)

            def halve(t, s):
                v = prod[:, s % 2, :, :]
                n, m = NSLOT - HALF, NSLOT - HALF - len(fields(ACT_Q[-1]))
                dve.wait_ge(act_done, t * len(ACT_Q) + (len(ACT_Q) - 1))
                dve.wait_ge(dve_done, t * len(DVE_Q) + len(DVE_Q))
                nc.vector.tensor_tensor(v[:, 0:m, :], v[:, 0:m, :], v[:, HALF:HALF + m, :], ALU.add).then_inc(halved, 1)
                dve.wait_ge(act_done, t * len(ACT_Q) + len(ACT_Q))
                nc.vector.tensor_tensor(v[:, m:n, :], v[:, m:n, :], v[:, HALF + m:NSLOT, :], ALU.add).then_inc(halved, 1)

            def body(turn, gi, turns, last):
                g = turn * TG + gi
                for n in range(1, GT if last else GT + 1):
                    t, s = g * GT + n, n % GT
                    for k in range(len(DVE_Q)):
                        fused(t, s, k, bank(("T", n, DVE_Q[k]), turns, last))
                        at = (n - 1) * len(DVE_Q) + k
                        if last:
                            continue
                        if turns and at == SPLIT_AFTER:
                            split_e(turn + 1)
                        for j in range(NJ):
                            if PRODUCT_AFTER[turns][j] == at:
                                pair_product(g + 1, j, bank(("B", j), turns))
                            if ZLO_AFTER[turns][j] == at:
                                zlo_out(g + 1, j)
                        for i in range(len(PIECES)):
                            if at == CLO_AFTER[i]:
                                clo_out(g + 1, i)
                        if at == SUM_AFTER:
                            sum_cur0(g + 1)
                    halve(t, s)

            dve.sem_inc(zlo_done, NJ)
            dve.wait_ge(const_in, 16)
            nc.vector.tensor_copy(ident[:, :], c_stage[:, C_ID:C_ID + P]).then_inc(consts_done, 1)
            nc.vector.tensor_copy(mask[:, :], c_stage[:, C_MASK:C_MASK + B8]).then_inc(consts_done, 1)
            nc.vector.tensor_copy(sel[:, :], c_stage[:, C_SEL:NC_CONST]).then_inc(consts_done, 1)
            dve.wait_ge(w0_in, 32)
            nc.vector.tensor_tensor(w0b_st[0:NPAIR, :], w0a_st[0:NPAIR, :], w0b_st[0:NPAIR, :], ALU.add).then_inc(w0_added, 1)
            dve.wait_ge(w0_added, 1)
            nc.vector.tensor_copy(w0hi[:, :], w0b_st).then_inc(w0_folded, 1)
            dve.wait_ge(w0_folded, 1)
            nc.vector.tensor_tensor(w0lo[:, :], w0b_st, w0hi[:, :].bitcast(F32), ALU.subtract).then_inc(w0_folded, 1)
            dve.wait_ge(w0_folded, 2)
            last_copy = (slice(COPIES[1], COPIES[1] + NREST), slice((NJ - 1) * H, NJ * H))
            nc.vector.tensor_copy(w0hi[last_copy], w0lo[last_copy].bitcast(F32)).then_inc(w0_done, 1)
            dve.wait_ge(w1hi_done, 1)
            nc.vector.tensor_tensor(w1lo[:, :], w1_stage, w1hi[:, :].bitcast(F32), ALU.subtract).then_inc(w1lo_done, 1)
            dve.wait_ge(padded, 1)
            nc.vector.tensor_copy(e2[:, :, NF:LO], a3[:, 0:D * (LO - NF)].rearrange("p (d k) -> p d k", d=D)).then_inc(e2_padded, 1)
            dve.wait_ge(gathered_early, 16 * EARLY)
            split_fields(0, EARLY, 1)
            dve.wait_ge(gathered_late, 16 * (NF - EARLY))
            split_fields(EARLY, NF, 2).then_inc(e2_done, 1)
            for j in range(NJ):
                pair_product(0, j, (6 + j) % NR)
            clo_out(0, 0)
            clo_out(0, 1)
            sum_cur0(0)
            clo_out(0, 2)
            for k in range(len(DVE_Q)):
                fused(0, 0, k, TAIL["T", GT, DVE_Q[k]] % NR)
            halve(0, 0)
            walk(dve, body)

        @block.tensor
        def _(pe):
            def freed(x, g, n0=0, turn=0):
                if x[0] == "T":
                    t, q = g * GT + (x[1] - n0), x[2]
                    if q in ACT_Q:
                        pe.wait_ge(act_done, t * len(ACT_Q) + (ACT_Q.index(q) + 1))
                    else:
                        pe.wait_ge(dve_done, t * len(DVE_Q) + (DVE_Q.index(q) + 1))
                elif x[0] == "S":
                    pe.wait_ge(s_done, g * GT + (x[1] - n0 + START))
                elif x[0] == "X":
                    pe.wait_ge(xt_done, turn * 4 + (4 + x[1] + 1))
                elif x[0] == "A":
                    pe.wait_ge(a3_done, g + 2)
                elif x[0] == "B":
                    pe.wait_ge(z_done, g * NJ + (NJ + x[1] + 1))
                elif x[0] == "R":
                    pe.wait_ge(xrn_done, g + 2)

            def transposes(turn, n, to):
                pe.wait_ge(e2_done, turn + 1)
                for i in range(4):
                    ins = nc.tensor.matmul(to[0:KX, i * P:(i + 1) * P], e2[:, 4 * n + i, :], ident[:, :],
                                           start=True, stop=True, skip_group_check=True)
                ins.then_inc(xt_mm, 1)

            def spread_a(g, b):
                pe.wait_ge(xs_done, g + 1)
                nc.tensor.matmul(ring[0:NPAIR, b, :], sel[0:KX, 0:NPAIR], xs[0:KX, :],
                                 start=True, stop=True).then_inc(a3_mm, 1)

            def row_major(g, b):
                for i in range(GT):
                    ins = nc.tensor.matmul(ring[:, b, i * F1:(i + 1) * F1], xs[0:KX, i * P:(i + 1) * P], selx,
                                           start=True, stop=True, skip_group_check=True)
                ins.then_inc(xr_mm, 1)

            def spread_b(g, j, b):
                c = (1 + j) * NPAIR
                nc.tensor.matmul(ring[0:NPAIR, b, :], sel[0:KX, c:c + NPAIR], xs[0:KX, :],
                                 start=True, stop=True).then_inc(b_mm, 1)

            def contract0(g, j):
                if j == 0:
                    pe.wait_ge(clo_done, g * len(PIECES))
                pe.wait_ge(zlo_done, g * NJ + (j + 1))
                m = slice(j * H, (j + 1) * H)
                if j == NJ - 1:
                    nc.tensor.matmul(cur0_ps[:, :], w0hi[0:LASTP, m], zhi[0:LASTP, j % NZ, :],
                                     start=False, stop=True).then_inc(z_used, 1)
                    return
                nc.tensor.matmul(cur0_ps[:, :], w0hi[:, m], zhi[:, j % NZ, :], start=(j == 0), stop=False)
                nc.tensor.matmul(cur0_ps[:, :], w0lo[:, m], zhi[:, j % NZ, :], start=False, stop=False)
                nc.tensor.matmul(cur0_ps[:, :], w0hi[:, m], zlo[:, j % NZ, :], start=False, stop=False).then_inc(z_used, 1)

            def contract_first(j):
                pe.wait_ge(z_done, j + 1)
                n = P if j < NJ - 1 else NREST
                nc.tensor.matmul(cur0_ps[:, :], w0b_st[0:n, j * H:(j + 1) * H], z[0:n, j % 2, :],
                                 start=(j == 0), stop=(j == NJ - 1)).then_inc(z_used, 1)

            def contract1(s, q, b):
                c = slice(s * P, (s + 1) * P)
                w = slice(FQ * q * H, (fields(q)[-1] + 1) * H)
                o = ring[:, b, 0:w.stop - w.start]
                nc.tensor.matmul(o, chi[:, c], w1hi[:, w], start=True, stop=False)
                nc.tensor.matmul(o, chi[:, c], w1lo[:, w], start=False, stop=False)
                nc.tensor.matmul(o, clo[:, c], w1hi[:, w], start=False, stop=True).then_inc(t_ready, 1)

            def contract_d(t, s, b):
                u = s % 2
                pe.wait_ge(cur1_done, t + (START + 1))
                pe.wait_ge(xbd_done, t + 1)
                nc.tensor.matmul(ring[:, b, 0:F1 * B8], cur1[:, u, :], xbd[:, u, :, :].rearrange("p f b -> p (f b)"),
                                 start=True, stop=True).then_inc(s_mm, 1)

            def layer2(n):
                for f in range(NF):
                    ins = nc.tensor.matmul(cur0_ps[:, 0:n], w2_sb[:, f, :], s_sb[:, f, 0:n],
                                           start=(f == 0), stop=(f == NF - 1))
                ins.then_inc(out2_mm, 1)

            def layer2_turns():
                pe.wait_ge(clo_done, len(PIECES) * (NG - TG + 1))
                pe.wait_ge(s_done, (NG - TG) * GT + START)
                layer2(B - P)

            def hidden1(w, x, first=False, last=False, ns=range(HID1 // P)):
                for n in ns:
                    ins = nc.tensor.matmul(h1_ps[n], w[:, n * P:(n + 1) * P], x, start=first, stop=last)
                    if last:
                        ins.then_inc(h1_mm, 1)

            def body(turn, gi, turns, last):
                g = turn * TG + gi
                steps, place = PLANS[2 if last else int(turns)]
                holder = {v % NR: (k, 0) for k, v in TAIL.items() if v >= -NR}
                for x in steps:
                    b = place[x] % NR if x in place else None
                    if x in place:
                        y, ended = holder[b]
                        freed(y, g, 0 if ended else GT, turn)
                        holder[b] = (x, 1)
                    if x[0] == "T":
                        n, q = x[1:]
                        for i, (lo, hi) in enumerate(PIECES):
                            if q == 0 and lo == n % GT:
                                pe.wait_ge(clo_done, (g + n // GT) * len(PIECES) + (i + 1))
                        contract1(n % GT, q, b)
                    elif x[0] == "S":
                        contract_d(g * GT + (x[1] - 1), x[1] - 1, b)
                    elif x[0] == "X":
                        if b is None:
                            pe.wait_ge(clo_done, (g + 2) * len(PIECES))
                        transposes(turn + 1, x[1], cur0_ps if b is None else ring[:, b, :])
                    elif x[0] == "A":
                        spread_a(g + 1, b)
                    elif x[0] == "B":
                        spread_b(g + 1, x[1], b)
                    elif x[0] == "R":
                        row_major(g + 1, b)
                    else:
                        contract0(g + 1, x[1])

            def keep_warm(n):
                for _ in range(n):
                    nc.tensor.matmul(cur0_ps[:, :], sel[:, 0:P], sel[:, 0:512], start=True, stop=True)

            pe.sem_inc(s_mm, START)
            pe.wait_ge(consts_done, 3)
            pe.wait_ge(gathered_early, 16 * EARLY)
            keep_warm(WARM_PRODUCTS[0])
            pe.wait_ge(e2_padded, 1)
            for n in range(D // 4):
                transposes(0, n, ring[:, n, :])
            keep_warm(WARM_PRODUCTS[1])
            spread_a(0, 4)
            row_major(0, 5)
            for j in range(5):
                spread_b(0, j, (6 + j) % NR)
            keep_warm(WARM_PRODUCTS[2])
            pe.wait_ge(w0_done, 1)
            for j in range(NJ):
                contract_first(j)
                if j == 0:
                    pe.wait_ge(a3_done, 1)
                    spread_b(0, 5, 4)
                if j == 1:
                    pe.wait_ge(xrn_done, 1)
                    spread_b(0, 6, 5)
            pe.wait_ge(clo_done, 1)
            pe.wait_ge(w1lo_done, 1)
            for q in range(NQ):
                y = next((r for r in range(q) if (TAIL["T", GT, q] - TAIL["T", GT, r]) == NR), None)
                if y is not None:
                    freed(("T", 0, y), 0)
                contract1(0, q, TAIL["T", GT, q] % NR)
            pe.wait_ge(w2_in, 16)
            walk(pe, body, layer2_turns)
            pe.wait_ge(top_in, 7 * 16)
            pe.wait_ge(summed0, NG)
            pe.wait_ge(act_done, NG * GT * len(ACT_Q) - sum(q > 7 for q in ACT_Q))
            pe.wait_ge(dve_done, NG * GT * len(DVE_Q) - sum(q > 7 for q in DVE_Q))
            for n in range(HID1 // P):
                if n == HID1 // P - 1:
                    contract_d(NG * GT - 1, GT - 1, top_bank(4))
                hidden1(wt1_sb[:, 0, :], z0t[:, :], first=True, ns=(n,))
                hidden1(wt1d_sb, dt_sb, ns=(n,))
            pe.wait_ge(s_done, NG * GT + START)
            layer2(P)
            pe.wait_ge(z1_done, 2)
            hidden1(wt1_sb[:, 1, :], z1t)
            pe.wait_ge(out2_done, 2)
            hidden1(wt1_sb[:, 2, :], z2t, last=True)
            for n in range(HID2 // P):
                for k in range(HID1 // P):
                    if n == 0:
                        pe.wait_ge(h1_done, k + 1)
                    ins = nc.tensor.matmul(h2_ps[n], wt2_sb[:, k, n * P:(n + 1) * P], h1t[:, k, :],
                                           start=(k == 0), stop=(k == HID1 // P - 1))
                ins.then_inc(h2_mm, 1)
            for k in range(HID2 // P):
                pe.wait_ge(h2_done, k + 1)
                ins = nc.tensor.matmul(y_ps, wt3_sb[:, k:k + 1], h2t[:, k, :],
                                       start=(k == 0), stop=(k == HID2 // P - 1))
            ins.then_inc(y_mm, 1)


def _pairs():
    first = [None] * P
    for f in range(NREST):
        for c in COPIES:
            first[c + f] = f
    others = [f for _ in range(P) for f in range(NREST, NF)]
    for p in range(P):
        if first[p] is None:
            first[p] = others.pop(0)
    room = [first.count(f) * (NJ - 1) + (f < NREST) for f in range(NF)]
    given = {f: [] for f in range(NF)}

    def give(f, g, seen):
        for a, b in ((f, g), (g, f)):
            if a not in seen:
                seen.add(a)
                if len(given[a]) < room[a]:
                    given[a].append(b)
                    return True
                for c in given[a]:
                    if c not in seen and c != a:
                        given[a].remove(c)
                        given[a].append(b)
                        if give(c, a, seen):
                            return True
                        given[a].remove(b)
                        given[a].append(c)
        return False

    for f in range(NF):
        given[f].append(f)
    for k in range(1, (NF + 1) // 2):
        for f in range(NF):
            assert give(f, (f + k) % NF, set())
    second = [[None] * P for _ in range(NJ)]
    for f in range(NREST):
        g = given[f].pop()
        for c in COPIES:
            second[NJ - 1][c + f] = g
    for j in range(NJ - 1):
        for p in range(P):
            second[j][p] = given[first[p]].pop()
    return first, second


def _constants():
    import numpy as np
    c = np.zeros((P, NC_CONST), np.float32)
    c[:, C_ID:C_ID + P] = np.eye(P)
    for row in range(P):
        c[row, C_MASK + row % B8] = 1.0
    first, second = _pairs()
    for p in range(P):
        for r in (first[p], LO + first[p]):
            c[r, C_SEL + p] = 1.0
        for j in range(NJ):
            if second[j][p] is not None:
                for r in (second[j][p], LO + second[j][p]):
                    c[r, C_SEL + (1 + j) * NPAIR + p] = 1.0
    for f in range(NF):
        for r in (f, LO + f):
            c[r, C_SELX + f] = 1.0
    return c


def kernel(**inputs):
    import numpy as np
    import concourse.bacc as bacc
    from concourse.bass_utils import run_bass_kernel_spmd

    f0 = np.asarray(inputs["L0_rec_f0"])
    w0a = np.zeros((P, NJ, H), f0.dtype)
    w0b = np.zeros((P, NJ, H), f0.dtype)
    first, second = _pairs()
    for j in range(NJ):
        for p in range(P):
            f, g = first[p], second[j][p]
            if g is not None:
                w0a[p, j] = f0[f * NF + g]
                if f != g:
                    w0b[p, j] = f0[g * NF + f]

    nc = bacc.Bacc("TRN2", target_bir_lowering=False, num_devices=1)
    arrays = {}

    def dram(name, a):
        a = np.ascontiguousarray(a)
        arrays[name] = a
        return nc.dram_tensor(name, a.shape, mybir.dt.from_np(a.dtype), kind="ExternalInput").ap()

    def by_partition(a):
        return np.asarray(a).reshape(-1, P).T

    args = [
        dram("ids", inputs["ids"]),
        [dram(f"tbl_{f}", inputs[f"tbl_{f}"]) for f in range(NF)],
        dram("consts", _constants()),
        dram("w0a", w0a), dram("w0b", w0b),
        dram("w1", inputs["L0_rec_f1"]), dram("w2", inputs["L0_rec_f2"]),
        dram("dense_t", np.asarray(inputs["dense_ctx"]).T),
        dram("w_top1", inputs["W_top1"]), dram("b_top1", by_partition(inputs["b_top1"])),
        dram("w_top2", inputs["W_top2"]), dram("b_top2", by_partition(inputs["b_top2"])),
        dram("w_top3", by_partition(inputs["W_top3"])),
        nc.dram_tensor("y", (1, B), F32, kind="ExternalOutput").ap(),
    ]
    build(nc, *args)
    return run_bass_kernel_spmd(nc, [arrays], core_ids=[0]).results[0]["y"].reshape(B, 1)
```
